# Optimizing a Trainium2 kernel written in Bass

```python
import numpy as np
import jax
import jax.numpy as jnp

def _softmax(x, axis=-1):
    return jax.nn.softmax(x, axis=axis)

def _gelu(x):
    return jax.nn.gelu(x, approximate=True)

def _silu(x):
    return jax.nn.silu(x)

def _sigmoid(x):
    return jax.nn.sigmoid(x)

def _layernorm(x, axis=-1, eps=1e-05):
    m = jnp.mean(x, axis=axis, keepdims=True)
    v = jnp.var(x, axis=axis, keepdims=True)
    return (x - m) / jnp.sqrt(v + eps)

def _scatter_add(tgt, idx, src, axis=0):
    return tgt.at[idx].add(src)

def _segment_sum(src, seg, n):
    return jax.ops.segment_sum(src, seg, n)
kernel_name = 'mk_adj_preln_d4_adj_r2_863711'

def setup_inputs(seed: int=0):
    np.random.seed(seed)
    _w = jnp.asarray

    def _rec_inputs():
        import jax
        import jax.numpy as jnp
        _gk = jax.random.key(seed)
        x = -0.0002928 + 1 * jax.random.normal(jax.random.fold_in(_gk, 1), (32, 256, 256), jnp.float32)
        _a = jax.random.bernoulli(jax.random.fold_in(_gk, 2), 0.015625, (32, 256, 256))
        _a = jnp.logical_or(_a, jnp.swapaxes(_a, -1, -2))
        _a = jnp.logical_or(_a, jnp.eye(256, dtype=bool))
        adj = _a.astype(jnp.int32)
        return (x, adj)
    x, adj = _rec_inputs()

    def _L0_gnn_setup():
        import jax, jax.numpy as jnp
        import numpy as np
        ALPHA = 0.2

        def _leaky(x):
            return jnp.where(x >= 0, x, ALPHA * x)
        key = jax.random.key(seed)
        k1, k2, k3, k4 = jax.random.split(key, 4)
        B, N, F_in, F_out = (4, 1024, 256, 256)
        h = jax.random.normal(k1, (B, N, F_in), dtype=jnp.float32)
        W = jax.random.normal(k2, (F_in, F_out), dtype=jnp.float32) * 0.05
        a = jax.random.normal(k3, (2 * F_out, 1), dtype=jnp.float32) * 0.05
        adj = jax.random.randint(k4, (B, N, N), 0, 2, dtype=jnp.int32)
        return {'h': h, 'W': W, 'a': a, 'adj': adj}
    _L0_gnn_all = _L0_gnn_setup()
    _L0_gnn_in = {k: v for k, v in _L0_gnn_all.items() if k in ('W', 'a')}
    del _L0_gnn_all

    def _L1_gnn_setup():
        import jax, jax.numpy as jnp
        import numpy as np
        B, N, D = (8, 512, 256)
        NH = 8
        DK = D // NH
        key = jax.random.key(seed)
        ks = jax.random.split(key, 6)
        x = jax.random.normal(ks[0], (B, N, D), dtype=jnp.float32)
        adj = jax.random.randint(ks[1], (B, N, N), 0, 2, dtype=jnp.int32)
        adj = jnp.maximum(adj, jnp.eye(N, dtype=jnp.int32)[None])
        s = 1.0 / np.sqrt(D)
        Wq = jax.random.normal(ks[2], (D, D), dtype=jnp.float32) * s
        Wk = jax.random.normal(ks[3], (D, D), dtype=jnp.float32) * s
        Wv = jax.random.normal(ks[4], (D, D), dtype=jnp.float32) * s
        Wo = jax.random.normal(ks[5], (D, D), dtype=jnp.float32) * s
        return {'x': x, 'adj': adj, 'Wq': Wq, 'Wk': Wk, 'Wv': Wv, 'Wo': Wo}
    _L1_gnn_all = _L1_gnn_setup()
    _L1_gnn_in = {k: v for k, v in _L1_gnn_all.items() if k in ('Wq', 'Wk', 'Wv', 'Wo')}
    del _L1_gnn_all

    def _L2_gnn_setup():
        import jax, jax.numpy as jnp
        import numpy as np
        NEG_INF = -1000000000.0
        NEG_SLOPE = 0.2

        def gat_layer(x, mask, W, a_src, a_dst, bias, concat):
            B, N, _ = x.shape
            H, F = a_src.shape
            xl = (x @ W).reshape(B, N, H, F)
            asrc = jnp.einsum('bnhf,hf->bnh', xl, a_src)
            adst = jnp.einsum('bnhf,hf->bnh', xl, a_dst)
            e = jax.nn.leaky_relu(asrc[:, :, None, :] + adst[:, None, :, :], NEG_SLOPE)
            e = jnp.where(mask[..., None], e, NEG_INF)
            attn = jax.nn.softmax(e, axis=1)
            out = jnp.einsum('bsdh,bshf->bdhf', attn, xl)
            if concat:
                out = out.reshape(B, N, H * F)
            else:
                out = out.mean(axis=2)
            return out + bias
        key = jax.random.key(seed)
        ks = jax.random.split(key, 10)
        B, N, Din, Fh, H, Dout = (8, 512, 256, 128, 4, 256)
        s = 0.05
        return {'adj': jax.random.randint(ks[0], (B, N, N), 0, 2, dtype=jnp.int32), 'x': jax.random.normal(ks[1], (B, N, Din), dtype=jnp.float32), 'W1': jax.random.normal(ks[2], (Din, H * Fh), dtype=jnp.float32) * s, 'att_src1': jax.random.normal(ks[3], (H, Fh), dtype=jnp.float32) * s, 'att_dst1': jax.random.normal(ks[4], (H, Fh), dtype=jnp.float32) * s, 'b1': jax.random.normal(ks[5], (H * Fh,), dtype=jnp.float32) * s, 'W2': jax.random.normal(ks[6], (H * Fh, Dout), dtype=jnp.float32) * s, 'att_src2': jax.random.normal(ks[7], (1, Dout), dtype=jnp.float32) * s, 'att_dst2': jax.random.normal(ks[8], (1, Dout), dtype=jnp.float32) * s, 'b2': jax.random.normal(ks[9], (Dout,), dtype=jnp.float32) * s}
    _L2_gnn_all = _L2_gnn_setup()
    _L2_gnn_in = {k: v for k, v in _L2_gnn_all.items() if k in ('W1', 'att_src1', 'att_dst1', 'b1', 'W2', 'att_src2', 'att_dst2', 'b2')}
    del _L2_gnn_all

    def _L3_gnn_setup():
        import jax, jax.numpy as jnp
        import numpy as np
        NEG_SLOPE = 0.2
        key = jax.random.key(seed)
        k1, k2, k3, k4, k5 = jax.random.split(key, 5)
        B, N, H = (8, 512, 256)
        node_features = jax.random.normal(k1, (B, N, H), dtype=jnp.float32)
        adjacency_matrix = jax.random.randint(k2, (B, N, N), 0, 2, dtype=jnp.int32)
        scale = 1.0 / np.sqrt(2 * H)
        attn_w_src = jax.random.uniform(k3, (H,), jnp.float32, -scale, scale)
        attn_w_dst = jax.random.uniform(k4, (H,), jnp.float32, -scale, scale)
        attn_b = jax.random.uniform(k5, (1,), jnp.float32, -scale, scale)
        return {'node_features': node_features, 'adjacency_matrix': adjacency_matrix, 'attn_w_src': attn_w_src, 'attn_w_dst': attn_w_dst, 'attn_b': attn_b}
    _L3_gnn_all = _L3_gnn_setup()
    _L3_gnn_in = {k: v for k, v in _L3_gnn_all.items() if k in ('attn_w_src', 'attn_w_dst', 'attn_b')}
    del _L3_gnn_all
    return {'x': x, 'adj': adj, 'L0_gnn_W': _L0_gnn_in['W'], 'L0_gnn_a': _L0_gnn_in['a'], 'L1_gnn_Wq': _L1_gnn_in['Wq'], 'L1_gnn_Wk': _L1_gnn_in['Wk'], 'L1_gnn_Wv': _L1_gnn_in['Wv'], 'L1_gnn_Wo': _L1_gnn_in['Wo'], 'L2_gnn_W1': _L2_gnn_in['W1'], 'L2_gnn_att_src1': _L2_gnn_in['att_src1'], 'L2_gnn_att_dst1': _L2_gnn_in['att_dst1'], 'L2_gnn_b1': _L2_gnn_in['b1'], 'L2_gnn_W2': _L2_gnn_in['W2'], 'L2_gnn_att_src2': _L2_gnn_in['att_src2'], 'L2_gnn_att_dst2': _L2_gnn_in['att_dst2'], 'L2_gnn_b2': _L2_gnn_in['b2'], 'L3_gnn_attn_w_src': _L3_gnn_in['attn_w_src'], 'L3_gnn_attn_w_dst': _L3_gnn_in['attn_w_dst'], 'L3_gnn_attn_b': _L3_gnn_in['attn_b']}

def reference(x, adj, L0_gnn_W, L0_gnn_a, L1_gnn_Wq, L1_gnn_Wk, L1_gnn_Wv, L1_gnn_Wo, L2_gnn_W1, L2_gnn_att_src1, L2_gnn_att_dst1, L2_gnn_b1, L2_gnn_W2, L2_gnn_att_src2, L2_gnn_att_dst2, L2_gnn_b2, L3_gnn_attn_w_src, L3_gnn_attn_w_dst, L3_gnn_attn_b):
    import jax
    import jax.numpy as jnp

    def _L0_gnn_ref(h, W, a, adj):
        import jax, jax.numpy as jnp
        import numpy as np
        ALPHA = 0.2

        def _leaky(x):
            return jnp.where(x >= 0, x, ALPHA * x)
        F_out = W.shape[1]
        Wh = jnp.matmul(h, W)
        Wh_sg = jax.lax.stop_gradient(Wh)
        a1 = a[:F_out, 0]
        a2 = a[F_out:, 0]
        s_i = Wh_sg @ a1
        s_j = Wh_sg @ a2
        e = _leaky(s_i[:, :, None] + s_j[:, None, :])
        e = jnp.where(adj > 0, e, jnp.float32(-9000000000000000.0))
        attention = jax.nn.softmax(e, axis=1)
        h_prime = jnp.einsum('bij,bjf->bif', attention, Wh)
        return _leaky(h_prime)

    def _L1_gnn_ref(x, adj, Wq, Wk, Wv, Wo):
        import jax, jax.numpy as jnp
        import numpy as np
        B, N, D = (8, 512, 256)
        NH = 8
        DK = D // NH
        b, n, d = x.shape
        sqrt_dk = jnp.asarray(np.sqrt(DK), dtype=x.dtype)

        def heads(t):
            return t.reshape(b, n, NH, DK).transpose(0, 2, 1, 3)
        q = heads(x @ Wq)
        k = heads(x @ Wk)
        v = heads(x @ Wv)
        scores = jnp.einsum('bhnd,bhmd->bhnm', q, k) / sqrt_dk
        mask = adj.astype(bool)[:, None]
        scores = jnp.where(mask, scores, -jnp.inf)
        attn = jax.nn.softmax(scores, axis=-1)
        out = jnp.einsum('bhnm,bhmd->bhnd', attn, v)
        out = out.transpose(0, 2, 1, 3).reshape(b, n, d)
        return jax.nn.relu(out) @ Wo

    def _L2_gnn_ref(adj, x, W1, att_src1, att_dst1, b1, W2, att_src2, att_dst2, b2):
        import jax, jax.numpy as jnp
        import numpy as np
        NEG_INF = -1000000000.0
        NEG_SLOPE = 0.2

        def gat_layer(x, mask, W, a_src, a_dst, bias, concat):
            B, N, _ = x.shape
            H, F = a_src.shape
            xl = (x @ W).reshape(B, N, H, F)
            asrc = jnp.einsum('bnhf,hf->bnh', xl, a_src)
            adst = jnp.einsum('bnhf,hf->bnh', xl, a_dst)
            e = jax.nn.leaky_relu(asrc[:, :, None, :] + adst[:, None, :, :], NEG_SLOPE)
            e = jnp.where(mask[..., None], e, NEG_INF)
            attn = jax.nn.softmax(e, axis=1)
            out = jnp.einsum('bsdh,bshf->bdhf', attn, xl)
            if concat:
                out = out.reshape(B, N, H * F)
            else:
                out = out.mean(axis=2)
            return out + bias
        B, N, _ = adj.shape
        mask = (adj > 0) | jnp.eye(N, dtype=bool)[None]
        h = jax.nn.elu(gat_layer(x, mask, W1, att_src1, att_dst1, b1, concat=True))
        h = gat_layer(h, mask, W2, att_src2, att_dst2, b2, concat=False)
        return h

    def _L3_gnn_ref(node_features, adjacency_matrix, attn_w_src, attn_w_dst, attn_b):
        import jax, jax.numpy as jnp
        import numpy as np
        NEG_SLOPE = 0.2
        B, N, H = node_features.shape
        s_src = jnp.einsum('bnh,h->bn', node_features, attn_w_src)
        s_dst = jnp.einsum('bnh,h->bn', node_features, attn_w_dst)
        scores = s_src[:, :, None] + s_dst[:, None, :] + attn_b[0]
        scores = jax.nn.leaky_relu(scores, negative_slope=NEG_SLOPE)
        adj = adjacency_matrix.astype(jnp.float32) + jnp.eye(N, dtype=jnp.float32)[None]
        scores = jnp.where(adj == 0, -jnp.inf, scores)
        attn = jax.nn.softmax(scores, axis=-1)
        return jnp.einsum('bij,bjh->bih', attn, node_features)
    h = jnp.maximum(_layernorm(x, axis=-1), 0.0)
    x = x + _L0_gnn_ref(h, L0_gnn_W, L0_gnn_a, adj)
    h = jnp.maximum(_layernorm(x, axis=-1), 0.0)
    x = x + _L1_gnn_ref(h, adj, L1_gnn_Wq, L1_gnn_Wk, L1_gnn_Wv, L1_gnn_Wo)
    h = jnp.maximum(_layernorm(x, axis=-1), 0.0)
    x = x + _L2_gnn_ref(adj, h, L2_gnn_W1, L2_gnn_att_src1, L2_gnn_att_dst1, L2_gnn_b1, L2_gnn_W2, L2_gnn_att_src2, L2_gnn_att_dst2, L2_gnn_b2)
    h = jnp.maximum(_layernorm(x, axis=-1), 0.0)
    x = x + _L3_gnn_ref(h, adj, L3_gnn_attn_w_src, L3_gnn_attn_w_dst, L3_gnn_attn_b)
    return x

_drawn_inputs = setup_inputs


def setup_inputs(seed=0):
    import zlib

    import numpy as np

    out = dict(_drawn_inputs(seed))
    spreads = {}
    factors = {'L2_gnn_att_src1': 4.621,
     'L2_gnn_att_dst1': 23.765,
     'L2_gnn_att_src2': 8.0,
     'L2_gnn_att_dst2': 64.0,
     'L3_gnn_attn_w_src': 8.0,
     'L3_gnn_attn_w_dst': 4.011}
    for name, (base, spread) in spreads.items():
        noise = np.random.default_rng([zlib.crc32(name.encode()), seed]).standard_normal(out[name].shape)
        drawn = base * np.exp(spread * noise) if base else spread * noise
        out[name] = jnp.asarray(drawn.astype(out[name].dtype))
    for name, factor in factors.items():
        out[name] = (out[name] * factor).astype(out[name].dtype)
    return out
```

```python
import concourse.bass as bass
from concourse import mybir
from contextlib import ExitStack


def four_graph_layers(nc, x, adj, w0, a0, wq, wk, wv, wo, w1, att_src1, att_dst1, b1, w2, att_src2,
                      att_dst2, b2, w_src3, w_dst3, b3, out):
    fp32, bf16, i32 = mybir.dt.float32, mybir.dt.bfloat16, mybir.dt.int32
    ALU, ACT, AX = mybir.AluOpType, mybir.ActivationFunctionType, mybir.AxisListType

    P = 128
    G, N, D = x.shape
    T = N // P
    C = D // P
    PAIRS = G // 2
    SLOTS = (0, 1)
    HEADS1 = 8
    DK = D // HEADS1
    PER = P // DK
    HEADS2 = att_src1.shape[0]
    F2 = att_src1.shape[1]
    FH = HEADS2 * F2
    CH = FH // P
    SLOPE = 0.2
    EPS = 1e-5
    MASKED = -float(2 ** 53)
    LOWEST = -3.0e38
    ONE = D + 2

    with ExitStack() as ctx:
        def sb(name, shape, dt=fp32):
            return ctx.enter_context(nc.sbuf_tensor(name, shape, dt))

        def two(name, shape, dt=fp32):
            return [sb(f"{name}_{s}", shape, dt) for s in SLOTS]

        def sem(name):
            return ctx.enter_context(nc.semaphore(name))

        def sems(name):
            return [sem(f"{name}_{s}") for s in SLOTS]

        ident = sb("ident", [P, P])
        ident16 = sb("ident16", [P, P], bf16)
        w0_sb = sb("w0_sb", [P, C, ONE])
        wq_sb, wk_sb, wv_sb, wo_sb = (sb(n, [P, C, D]) for n in ("wq_sb", "wk_sb", "wv_sb", "wo_sb"))
        w1_sb = sb("w1_sb", [P, C, FH])
        w1_cols = sb("w1_cols", [P, C, HEADS2, 2])
        w2_sb = sb("w2_sb", [P, CH, ONE])
        wT_sb = sb("wT_sb", [P, 2, 512])
        a0_sb = sb("a0_sb", [P, C, 2])
        att1_sb = sb("att1_sb", [P, HEADS2, 2])
        att2_sb = sb("att2_sb", [P, C, 2])
        b1_bc = sb("b1_bc", [P, FH])
        b2_bc = sb("b2_bc", [P, D])
        w3_bc = sb("w3_bc", [P, 2, D])
        b3_bc = sb("b3_bc", [P, 1])
        minus_one = sb("minus_one", [P, 1])
        minus_half = sb("minus_half", [P, T])

        adj_in = two("adj_in", [P, T, N], i32)
        x_in = two("x_in", [P, T, D])
        x_run = two("x_run", [P, T, D])
        x_out = two("x_out", [P, T, D])
        bn = two("bn", [P, T, 6])
        mean_var = two("mean_var", [P, T, 2])
        var_eps = two("var_eps", [P, T])
        rstd = two("rstd", [P, T])
        hn = two("hn", [P, T, D])
        hT = two("hT", [P, C, N])
        mask_n = two("mask_n", [P, T, N], bf16)
        mask_t = two("mask_t", [P, T, N], bf16)
        val = two("val", [P, T, FH])
        cols = two("cols", [P, T, HEADS2, 2])
        z = two("z", [P, 4, T, N])
        row_max = two("row_max", [P, T, HEADS2])
        row_top = two("row_top", [P, T, HEADS2])
        row_low = two("row_low", [P, T, HEADS2])
        neg_max = two("neg_max", [P, T, HEADS2])
        neg_max1 = two("neg_max1", [P, HEADS1, T])
        row_sum = two("row_sum", [P, T, HEADS2])
        rec = two("rec", [P, T, HEADS2])
        row_sum1 = two("row_sum1", [P, T, HEADS1])
        rec1 = two("rec1", [P, T, HEADS1, DK])
        pT = two("pT", [P, 4, T, N])
        qT = two("qT", [P, C, N])
        kT = two("kT", [P, C, N])
        rec_bc = two("rec_bc", [P, C, N])
        oT = two("oT", [P, C, N])
        u = two("u", [P, T, FH])
        e = two("e", [P, T, FH])
        h1T = two("h1T", [P, CH, N])
        ps = [ctx.enter_context(nc.psum_tensor(f"ps_{s}", [P, 4, 512], fp32)) for s in SLOTS]

        def bank(s, b):
            return ps[s][:, b, :]

        def halves(s, b):
            return ps[s][:, b, :].rearrange("p (t n) -> p t n", t=2)

        consts_in = sem("consts_in")
        ident_made = sem("ident_made")
        setup_psum, setup_sb = sem("setup_psum"), sem("setup_sb")
        setup_done = sem("setup_done")
        adj_loaded, x_loaded, stored = sems("adj_loaded"), sems("x_loaded"), sems("stored")
        mask_n_made, mask_t_psum, mask_t_made = sems("mask_n_made"), sems("mask_t_psum"), sems("mask_t_made")
        mask_t_diag, mask_n_diag = sems("mask_t_diag"), sems("mask_n_diag")
        bn_done, mv_done = sems("bn_done"), sems("mv_done")
        var_done = sems("var_done")
        rstd_made, hn_made = sems("rstd_made"), sems("hn_made")
        hT_psum, hT_made = sems("hT_psum"), sems("hT_made")
        x_made = sems("x_made")
        proj, cols_made = sems("proj"), sems("cols_made")
        val_made = sems("val_made")
        bcast = sems("bcast")
        z_made, top_made, low_made, neg_made = sems("z_made"), sems("top_made"), sems("low_made"), sems("neg_made")
        scaled, leaky_done = sems("scaled"), sems("leaky_done")
        exp_done = sems("exp_done")
        rec_made = sems("rec_made")
        pT_psum = sems("pT_psum")
        pT_by_act, pT_by_dve = sems("pT_by_act"), sems("pT_by_dve")
        pv = sems("pv")
        low0, leaky0 = sems("low0"), sems("leaky0")
        q_psum, k_psum, v_psum = sems("q_psum"), sems("k_psum"), sems("v_psum")
        q_made, k_made, v_made = sems("q_made"), sems("k_made"), sems("v_made")
        s_psum, neg1_made, exp1_done = sems("s_psum"), sems("neg1_made"), sems("exp1_done")
        o_psum, r_psum, r_made, oT_made, wo_psum = (sems(n) for n in ("o_psum", "r_psum", "r_made", "oT_made", "wo_psum"))
        pv2, u_made, e_made, h1_made = sems("pv2"), sems("u_made"), sems("e_made"), sems("h1_made")
        h1T_psum, h1T_made = sems("h1T_psum"), sems("h1T_made")
        dve_passed, pool_passed = sem("dve_passed"), sem("pool_passed")
        relu3, raw3, out_made = sems("relu3"), sems("raw3"), sems("out_made")

        BY_ACT = {1, 3, 5, 7, 9, 11}
        CALLS = ((0, 1), (1, HEADS2), (1 + HEADS2, 1), (2 + HEADS2, 1))
        PT_OF = (None, HEADS1, HEADS1 + HEADS2, HEADS1 + HEADS2 + 1)
        REC_OF = (1, 3, 4, 5)

        ALL_PT = HEADS1 + HEADS2 + 2

        def wait_pT(eng, s, it, n):
            by_act = len([m for m in BY_ACT if m <= n])
            if by_act:
                eng.wait_ge(pT_by_act[s], len(BY_ACT) * it + by_act)
            if n + 1 - by_act:
                eng.wait_ge(pT_by_dve[s], (ALL_PT - len(BY_ACT)) * it + n + 1 - by_act)

        def held_until(eng, passed, semaphore, value):
            eng.wait_ge(semaphore, value)
            eng.sem_inc(passed, 1)

        x_v = x.rearrange("g (t p) d -> g p t d", p=P)
        adj_v = adj.rearrange("g (t p) n -> g p t n", p=P)
        out_v = out.rearrange("g (t p) d -> g p t d", p=P)

        block = ctx.enter_context(nc.Block())

        @block.sync
        def _(sp):
            for dst, src in ((w0_sb[:, :, 0:D], w0), (wq_sb[:], wq), (wk_sb[:], wk), (wv_sb[:], wv),
                             (wo_sb[:], wo), (w1_sb[:], w1), (w2_sb[:, :, 0:D], w2)):
                sp.dma_start(dst, src.rearrange("(c p) n -> p c n", p=P)).then_inc(consts_in, 16)
            with nc.allow_non_contiguous_dma(reason="vectors laid along the partitions, once"):
                for half in range(2):
                    sp.dma_start(a0_sb[:, :, half],
                                 a0[half * D:(half + 1) * D, 0].rearrange("(c p) -> p c", p=P)).then_inc(consts_in, 16)
                sp.dma_start(att1_sb[:, :, 0], att_src1.rearrange("h f -> f h")).then_inc(consts_in, 16)
                sp.dma_start(att1_sb[:, :, 1], att_dst1.rearrange("h f -> f h")).then_inc(consts_in, 16)
                sp.dma_start(att2_sb[:, :, 0], att_src2.rearrange("o (c p) -> p (o c)", p=P)).then_inc(consts_in, 16)
                sp.dma_start(att2_sb[:, :, 1], att_dst2.rearrange("o (c p) -> p (o c)", p=P)).then_inc(consts_in, 16)
            for dst, src in ((b1_bc[:], b1), (b2_bc[:], b2), (w3_bc[:, 0, :], w_dst3), (w3_bc[:, 1, :], w_src3),
                             (b3_bc[:], b3)):
                sp.dma_start(dst, src.partition_broadcast(P)).then_inc(consts_in, 16)

            def load(g, s):
                sp.dma_start(adj_in[s][:], adj_v[bass.ds(g, 1)].squeeze(0) if not isinstance(g, int) else adj_v[g]).then_inc(adj_loaded[s], 16)
                sp.dma_start(x_in[s][:], x_v[bass.ds(g, 1)].squeeze(0) if not isinstance(g, int) else x_v[g]).then_inc(x_loaded[s], 16)

            def store(g, s):
                sp.dma_start(out_v[bass.ds(g, 1)].squeeze(0) if not isinstance(g, int) else out_v[g], x_out[s][:]).then_inc(stored[s], 16)

            for s in SLOTS:
                load(s, s)
                sp.sem_inc(stored[s], 16)
            with sp.Fori(0, PAIRS - 1) as it:
                for s in SLOTS:
                    sp.wait_ge(mask_n_made[s], it + 1)
                    sp.wait_ge(x_made[s], 3 * it + 1)
                    load(2 * it + 2 + s, s)
                for s in SLOTS:
                    sp.wait_ge(out_made[s], it + 1)
                    store(2 * it + s, s)
            for s in SLOTS:
                sp.wait_ge(out_made[s], PAIRS)
                store(G - 2 + s, s)
            for s in SLOTS:
                sp.wait_ge(stored[s], 16 * (PAIRS + 1))

        @block.gpsimd
        def _(pool):
            nc.gpsimd.memset(ident[:], 0.0).then_inc(ident_made, 1)
            nc.gpsimd.memset(minus_one[:], -1.0)
            nc.gpsimd.memset(minus_half[:], -0.5)
            pool.wait_ge(ident_made, 1)
            nc.gpsimd.affine_select(out=ident[:], in_=ident[:], compare_op=ALU.not_equal, fill=1.0, base=0,
                                    pattern=[[-1, P]], channel_multiplier=1).then_inc(ident_made, 1)
            pool.wait_ge(ident_made, 2)
            nc.gpsimd.tensor_copy(ident16[:], ident[:]).then_inc(ident_made, 1)
            with pool.Fori(0, PAIRS) as it:
                for s in SLOTS:
                    held_until(pool, pool_passed, adj_loaded[s], 16 * it + 16)
                    nc.gpsimd.tensor_scalar(mask_n[s][:], adj_in[s][:], 0, MASKED, ALU.is_le,
                                            ALU.mult).then_inc(mask_n_made[s], 1)

                def inverse_std(s, layer):
                    held_until(pool, pool_passed, mv_done[s], 8 * it + 2 * layer + 2)
                    nc.gpsimd.tensor_scalar(var_eps[s][:], mean_var[s][:, :, 1], EPS, 1.0, ALU.add,
                                            ALU.mult).then_inc(var_done[s], 1)
                    pool.wait_ge(var_done[s], 4 * it + layer + 1)
                    nc.gpsimd.tensor_tensor(rstd[s][:], var_eps[s][:], minus_half[:],
                                            ALU.pow).then_inc(rstd_made[s], 1)

                def open_diagonal(mask, done):
                    for t in range(T):
                        v = mask[:, t, t * P:(t + 1) * P]
                        last = nc.gpsimd.affine_select(out=v, in_=v, compare_op=ALU.not_equal, fill=0.0, base=0,
                                                       pattern=[[-1, P]], channel_multiplier=1)
                    last.then_inc(done, 1)

                def scale_scores(s, call):
                    before, heads = CALLS[call]
                    held_until(pool, pool_passed, z_made[s], 4 * it + call + 1)
                    for h in range(heads):
                        for t in range(T):
                            last = nc.gpsimd.tensor_scalar(pT[s][:, h, t, :], z[s][:, h, t, :],
                                                           cols[s][:, t, h, 1:2], SLOPE, ALU.add, ALU.mult)
                        last.then_inc(scaled[s], 1)

                for s in SLOTS:
                    inverse_std(s, 0)
                for s in SLOTS:
                    scale_scores(s, 0)
                for s in SLOTS:
                    open_diagonal(mask_t[s], mask_t_diag[s])
                for s in SLOTS:
                    inverse_std(s, 1)
                for s in SLOTS:
                    held_until(pool, pool_passed, s_psum[s], 8 * it + HEADS1)
                    open_diagonal(mask_n[s], mask_n_diag[s])
                for s in SLOTS:
                    inverse_std(s, 2)
                for call in (1, 2):
                    for s in SLOTS:
                        scale_scores(s, call)
                for s in SLOTS:
                    inverse_std(s, 3)
                for s in SLOTS:
                    scale_scores(s, 3)
                for s in SLOTS:
                    pool.wait_ge(out_made[s], it + 1)

        @block.tensor
        def _(pe):
            mm, tr = nc.tensor.matmul, nc.tensor.transpose

            pe.wait_ge(consts_in, 16 * 18)
            pe.wait_ge(ident_made, 3)
            for f in range(C):
                for c in range(C):
                    last = tr(bank(0, f)[:, c * P:(c + 1) * P], w0_sb[:, c, f * P:(f + 1) * P], ident[:])
            last.then_inc(setup_psum, 1)
            pe.wait_ge(setup_sb, 1)
            for c in range(C):
                for f in range(C):
                    last = mm(bank(0, 2)[:, 2 * c:2 * c + 2], wT_sb[:, f, c * P:(c + 1) * P], a0_sb[:, f, :],
                              start=(f == 0), stop=(f == C - 1))
            last.then_inc(setup_psum, 1)
            for h in range(HEADS2):
                pe.wait_ge(setup_sb, 2 + h)
                for c in range(C):
                    last = tr(bank(0, 0)[:, c * P:(c + 1) * P], w1_sb[:, c, h * F2:(h + 1) * F2], ident[:])
                last.then_inc(setup_psum, 1)
                pe.wait_ge(setup_sb, 3 + h)
                for c in range(C):
                    last = mm(bank(0, 3)[:, (c * HEADS2 + h) * 2:(c * HEADS2 + h) * 2 + 2],
                              wT_sb[:, 0, c * P:(c + 1) * P], att1_sb[:, h, :], start=True, stop=True)
            last.then_inc(setup_psum, 1)
            for f in range(C):
                for c in range(CH):
                    last = tr(bank(1, f)[:, c * P:(c + 1) * P], w2_sb[:, c, f * P:(f + 1) * P], ident[:])
            last.then_inc(setup_psum, 1)
            pe.wait_ge(setup_sb, 4 + HEADS2)
            for c in range(CH):
                for f in range(C):
                    last = mm(bank(0, 2)[:, 2 * c:2 * c + 2], wT_sb[:, f, c * P:(c + 1) * P], att2_sb[:, f, :],
                              start=(f == 0), stop=(f == C - 1))
            last.then_inc(setup_psum, 1)
            pe.wait_ge(setup_done, 1)

            with pe.Fori(0, PAIRS) as it:
                def transpose_mask(s):
                    pe.wait_ge(mask_n_made[s], it + 1)
                    to = bank(s, 3).bitcast(bf16)
                    for t in range(T):
                        for r in range(T):
                            last = tr(to[:, t * N + r * P:t * N + (r + 1) * P],
                                      mask_n[s][:, r, t * P:(t + 1) * P], ident16[:])
                    last.then_inc(mask_t_psum[s], 1)

                def transpose_h(s, layer):
                    pe.wait_ge(hn_made[s], 4 * it + layer + 1)
                    for c in range(C):
                        for t in range(T):
                            last = tr(halves(s, 0)[:, c, t * P:(t + 1) * P], hn[s][:, t, c * P:(c + 1) * P], ident[:])
                    last.then_inc(hT_psum[s], 1)

                def project(s, left, n_in, w, width, b0):
                    for t in range(T):
                        for c in range(n_in):
                            last = mm(bank(s, b0 + t)[:, 0:width], left[:, c, t * P:(t + 1) * P], w[:, c, :],
                                      start=(c == 0), stop=(c == n_in - 1))
                    return last

                def broadcast_scores(s, call, cols_value):
                    before, heads = CALLS[call]
                    pe.wait_ge(cols_made[s], cols_value)
                    for h in range(heads):
                        to = halves(s, 0 if h < 2 else 3)[:, h % 2, :]
                        for t in range(T):
                            last = tr(to[:, t * P:(t + 1) * P],
                                      cols[s][:, t, h, 0:1].to_broadcast([P, P]), ident[:])
                        last.then_inc(bcast[s], 1)

                def transpose_p(s, b, slot_in_z, source_ready):
                    source_ready()
                    for m in range(T):
                        for t in range(T):
                            last = tr(halves(s, b)[:, m, t * P:(t + 1) * P],
                                      z[s][:, slot_in_z, t, m * P:(m + 1) * P], ident[:])
                    last.then_inc(pT_psum[s], 1)

                for s in SLOTS:
                    transpose_mask(s)
                for s in SLOTS:
                    transpose_h(s, 0)
                for s in SLOTS:
                    pe.wait_ge(hT_made[s], 3 * it + 1)
                    project(s, hT[s], C, w0_sb, ONE, 1).then_inc(proj[s], 1)
                for s in SLOTS:
                    broadcast_scores(s, 0, 4 * it + 1)
                for s in SLOTS:
                    pe.wait_ge(exp_done[s], 7 * it + 1)
                    pe.wait_ge(val_made[s], 3 * it + 1)
                    pe.wait_ge(mask_t_made[s], it + 1)
                    for i in range(T):
                        for j in range(T):
                            last = mm(halves(s, 3)[:, i, :], z[s][:, 0, j, i * P:(i + 1) * P],
                                      val[s][:, j, 0:D], start=(j == 0), stop=(j == T - 1))
                    last.then_inc(pv[s], 1)

                for s in SLOTS:
                    transpose_h(s, 1)
                for s in SLOTS:
                    pe.wait_ge(hT_made[s], 3 * it + 2)
                    for w, b, done in ((wq_sb, 1, q_psum), (wk_sb, 2, k_psum)):
                        for f in range(C):
                            for c in range(C):
                                last = mm(halves(s, b)[:, f, :], w[:, c, f * P:(f + 1) * P], hT[s][:, c, :],
                                          start=(c == 0), stop=(c == C - 1))
                        last.then_inc(done[s], 1)
                    for t in range(T):
                        for c in range(C):
                            last = mm(halves(s, 3)[:, t, :], hT[s][:, c, t * P:(t + 1) * P], wv_sb[:, c, :],
                                      start=(c == 0), stop=(c == C - 1))
                    last.then_inc(v_psum[s], 1)

                def scores1(s, h):
                    f, at = h // PER, DK * (h % PER)
                    if h >= 2:
                        pe.wait_ge(exp1_done[s], 8 * it + h - 1)
                    for t in range(T):
                        mm(halves(s, h % 2)[:, t, :], ident16[:], mask_n[s][:, t, :], start=True, stop=False)
                        last = mm(halves(s, h % 2)[:, t, :], qT[s][at:at + DK, f, t * P:(t + 1) * P],
                                  kT[s][at:at + DK, f, :], start=False, stop=True)
                    last.then_inc(s_psum[s], 1)

                def weighted_v(s, f):
                    wait_pT(pe, s, it, PER * (f + 1) - 1)
                    if f == 0:
                        pe.wait_ge(v_made[s], it + 1)
                    for m in range(T):
                        for j in range(PER):
                            h = PER * f + j
                            last = mm(halves(s, 3)[DK * j:DK * (j + 1), f, :], val[s][:, m, h * DK:(h + 1) * DK],
                                      pT[s][:, j, m, :], start=(m == 0), stop=(m == T - 1))
                    if f == C - 1:
                        last.then_inc(o_psum[s], 1)

                for h in (0, 1):
                    for s in SLOTS:
                        if h == 0:
                            pe.wait_ge(q_made[s], it + 1)
                            pe.wait_ge(k_made[s], it + 1)
                        scores1(s, h)
                for h in range(HEADS1):
                    for s in SLOTS:
                        def ready():
                            pe.wait_ge(exp1_done[s], 8 * it + h + 1)
                            if h:
                                wait_pT(pe, s, it, h - 1)
                        transpose_p(s, 2, h % 4, ready)
                        if h + 2 < HEADS1:
                            scores1(s, h + 2)
                    if h % PER == PER - 1:
                        for s in SLOTS:
                            weighted_v(s, h // PER)
                for s in SLOTS:
                    pe.wait_ge(rec_made[s], 5 * it + 2)
                    for f in range(C):
                        for t in range(T):
                            last = tr(halves(s, 0)[:, f, t * P:(t + 1) * P],
                                      rec1[s][:, t, PER * f:PER * (f + 1), :].rearrange("p h d -> p (h d)"),
                                      ident[:])
                    last.then_inc(r_psum[s], 1)
                for s in SLOTS:
                    pe.wait_ge(oT_made[s], it + 1)
                    for t in range(T):
                        for c in range(C):
                            last = mm(halves(s, 1)[:, t, :], oT[s][:, c, t * P:(t + 1) * P], wo_sb[:, c, :],
                                      start=(c == 0), stop=(c == C - 1))
                    last.then_inc(wo_psum[s], 1)

                for s in SLOTS:
                    transpose_h(s, 2)
                for s in SLOTS:
                    pe.wait_ge(hT_made[s], 3 * it + 3)
                    project(s, hT[s], C, w1_sb, FH, 1)
                    for t in range(T):
                        for c in range(C):
                            last = mm(bank(s, 3)[:, t * 2 * HEADS2:(t + 1) * 2 * HEADS2],
                                      hT[s][:, c, t * P:(t + 1) * P],
                                      w1_cols[:, c, :, :].rearrange("p h v -> p (h v)"),
                                      start=(c == 0), stop=(c == C - 1))
                    last.then_inc(proj[s], 1)
                for s in SLOTS:
                    broadcast_scores(s, 1, 4 * it + 2)

                def ready2(s, h):
                    pe.wait_ge(exp_done[s], 7 * it + 2 + h)
                    if h >= 2:
                        wait_pT(pe, s, it, HEADS1 + h - 2)

                def weighted2(s, h):
                    wait_pT(pe, s, it, HEADS1 + h)
                    for d in range(T):
                        for m in range(T):
                            last = mm(bank(s, 1 + d)[:, h * F2:(h + 1) * F2], pT[s][:, h, m, d * P:(d + 1) * P],
                                      val[s][:, m, h * F2:(h + 1) * F2], start=(m == 0), stop=(m == T - 1))
                    if h == HEADS2 - 1:
                        last.then_inc(pv2[s], 1)

                for h in range(HEADS2 + 1):
                    for s in SLOTS:
                        if h < HEADS2:
                            transpose_p(s, (0, 3)[h % 2], h, lambda: ready2(s, h))
                        if h == 1:
                            pe.wait_ge(val_made[s], 3 * it + 2)
                        if h >= 1:
                            weighted2(s, h - 1)

                for s in SLOTS:
                    pe.wait_ge(h1_made[s], it + 1)
                    for half in range(2):
                        for c in range(CH // 2):
                            for t in range(T):
                                last = tr(halves(s, (0, 3)[half])[:, c, t * P:(t + 1) * P],
                                          u[s][:, t, (CH // 2 * half + c) * P:(CH // 2 * half + c + 1) * P], ident[:])
                        last.then_inc(h1T_psum[s], 1)
                for s in SLOTS:
                    pe.wait_ge(h1T_made[s], 2 * it + 2)
                    project(s, h1T[s], CH, w2_sb, ONE, 1).then_inc(proj[s], 1)

                def weighted(s, call, rows, val_value):
                    wait_pT(pe, s, it, PT_OF[call])
                    if val_value is not None:
                        pe.wait_ge(val_made[s], val_value)
                    for d in range(T):
                        for m in range(T):
                            last = mm(halves(s, 1)[:, d, :], pT[s][:, 0, m, d * P:(d + 1) * P],
                                      rows[:, m, 0:D], start=(m == 0), stop=(m == T - 1))
                    last.then_inc(pv[s], 1)

                for s in SLOTS:
                    broadcast_scores(s, 2, 4 * it + 3)
                for s in SLOTS:
                    transpose_p(s, 3, 0, lambda: pe.wait_ge(exp_done[s], 7 * it + 6))
                for s in SLOTS:
                    weighted(s, 2, val[s], 3 * it + 3)

                for s in SLOTS:
                    broadcast_scores(s, 3, 4 * it + 4)
                for s in SLOTS:
                    transpose_p(s, 3, 0, lambda: pe.wait_ge(exp_done[s], 7 * it + 7))
                for s in SLOTS:
                    weighted(s, 3, hn[s], None)

        @block.scalar
        def _(act):
            fn = nc.scalar.activation
            with act.Fori(0, PAIRS) as it:
                def make_hT(s, layer):
                    act.wait_ge(hT_psum[s], 3 * it + layer + 1)
                    fn(hT[s][:], halves(s, 0), ACT.Relu).then_inc(hT_made[s], 1)

                def softmax(s, call):
                    before, heads = CALLS[call]
                    act.wait_ge(neg_made[s], 4 * it + call + 1)
                    for h in range(heads):
                        act.wait_ge(leaky_done[s], 7 * it + before + h + 1)
                        for t in range(T):
                            last = fn(z[s][:, h, t, :], z[s][:, h, t, :], ACT.Exp, bias=neg_max[s][:, t, h:h + 1],
                                      accum_out=row_sum[s][:, t, h:h + 1])
                        last.then_inc(exp_done[s], 1)

                def take_pT(s, n, b, to):
                    if n in BY_ACT:
                        act.wait_ge(pT_psum[s], 14 * it + n + 1)
                        fn(pT[s][:, to, :, :], halves(s, b), ACT.Copy).then_inc(pT_by_act[s], 1)

                for s in SLOTS:
                    act.wait_ge(mask_t_psum[s], it + 1)
                    fn(mask_t[s][:].rearrange("p t n -> p (t n)"), bank(s, 3).bitcast(bf16)[:, 0:T * N],
                       ACT.Copy).then_inc(mask_t_made[s], 1)
                for s in SLOTS:
                    make_hT(s, 0)
                for s in SLOTS:
                    softmax(s, 0)
                for s in SLOTS:
                    act.wait_ge(pv[s], 3 * it + 1)
                    fn(u[s][:, :, 0:D], halves(s, 3), ACT.Copy, scale=SLOPE).then_inc(low0[s], 1)
                for s in SLOTS:
                    make_hT(s, 1)
                for s in SLOTS:
                    act.wait_ge(q_psum[s], it + 1)
                    fn(qT[s][:], halves(s, 1), ACT.Copy, scale=float(DK) ** -0.5).then_inc(q_made[s], 1)
                    act.wait_ge(v_psum[s], it + 1)
                    fn(val[s][:, :, 0:D], halves(s, 3), ACT.Copy).then_inc(v_made[s], 1)

                def exp1(s, h):
                    act.wait_ge(neg1_made[s], 8 * it + h + 1)
                    for t in range(T):
                        last = fn(z[s][:, h % 4, t, :], halves(s, h % 2)[:, t, :], ACT.Exp,
                                  bias=neg_max1[s][:, h, t:t + 1], accum_out=row_sum1[s][:, t, h:h + 1])
                    last.then_inc(exp1_done[s], 1)

                for h in (0, 1):
                    for s in SLOTS:
                        exp1(s, h)
                for h in range(HEADS1):
                    for s in SLOTS:
                        take_pT(s, h, 2, h % 4)
                        if h + 2 < HEADS1:
                            exp1(s, h + 2)
                for s in SLOTS:
                    act.wait_ge(r_psum[s], it + 1)
                    fn(rec_bc[s][:], halves(s, 0), ACT.Copy).then_inc(r_made[s], 1)
                for s in SLOTS:
                    make_hT(s, 2)
                for s in SLOTS:
                    softmax(s, 1)
                for h in range(HEADS2):
                    for s in SLOTS:
                        take_pT(s, HEADS1 + h, (0, 3)[h % 2], h)
                for s in SLOTS:
                    act.wait_ge(u_made[s], it + 1)
                    fn(e[s][:], u[s][:], ACT.Exp, bias=minus_one[:]).then_inc(e_made[s], 1)
                for s in SLOTS:
                    for half in range(2):
                        act.wait_ge(h1T_psum[s], 2 * it + half + 1)
                        fn(h1T[s][:, CH // 2 * half:CH // 2 * (half + 1), :], halves(s, (0, 3)[half]), ACT.Identity,
                           bias=minus_one[:]).then_inc(h1T_made[s], 1)
                for s in SLOTS:
                    softmax(s, 2)
                for s in SLOTS:
                    take_pT(s, HEADS1 + HEADS2, 3, 0)
                for s in SLOTS:
                    softmax(s, 3)
                for s in SLOTS:
                    take_pT(s, HEADS1 + HEADS2 + 1, 3, 0)

        @block.vector
        def _(dve):
            v = nc.vector
            dve.wait_ge(setup_psum, 1)
            v.tensor_copy(wT_sb[:, :, 0:D], ps[0][:, 0:2, 0:D]).then_inc(setup_sb, 1)
            dve.wait_ge(setup_psum, 2)
            v.tensor_copy(w0_sb[:, :, D:D + 2],
                          bank(0, 2)[:, 0:2 * C].rearrange("p (c v) -> p c v", v=2)).then_inc(setup_sb, 1)
            for h in range(HEADS2):
                dve.wait_ge(setup_psum, 3 + h)
                v.tensor_copy(wT_sb[:, 0, 0:D], bank(0, 0)[:, 0:D]).then_inc(setup_sb, 1)
            dve.wait_ge(setup_psum, 3 + HEADS2)
            v.tensor_copy(w1_cols[:].rearrange("p c h v -> p (c h v)"),
                          bank(0, 3)[:, 0:C * HEADS2 * 2]).then_inc(setup_sb, 1)
            dve.wait_ge(setup_psum, 4 + HEADS2)
            v.tensor_copy(wT_sb[:, :, 0:FH], ps[1][:, 0:2, 0:FH]).then_inc(setup_sb, 1)
            dve.wait_ge(consts_in, 16 * 18)
            v.tensor_scalar(b1_bc[:], b1_bc[:], 1.0, None, ALU.add)
            dve.wait_ge(setup_psum, 5 + HEADS2)
            v.tensor_copy(w2_sb[:, :, D:D + 2],
                          bank(0, 2)[:, 0:2 * CH].rearrange("p (c v) -> p c v", v=2)).then_inc(setup_done, 1)
            dve.wait_ge(setup_done, 1)

            with dve.Fori(0, PAIRS) as it:
                def statistics(s, layer):
                    src = x_run[s] if layer else x_in[s]
                    if layer:
                        dve.wait_ge(x_made[s], 3 * it + layer)
                    else:
                        dve.wait_ge(x_loaded[s], 16 * it + 16)
                    for t in range(T):
                        v.bn_stats(bn[s][:, t, :], src[:, t, :]).then_inc(bn_done[s], 1)
                    for t in range(T):
                        held_until(dve, dve_passed, bn_done[s], 8 * it + 2 * layer + t + 1)
                        v.bn_aggr(mean_var[s][:, t, :], bn[s][:, t, :]).then_inc(mv_done[s], 1)

                def normalise(s, layer):
                    src = x_run[s] if layer else x_in[s]
                    dve.wait_ge(rstd_made[s], 4 * it + layer + 1)
                    for t in range(T):
                        last = v.tensor_scalar(hn[s][:, t, :], src[:, t, :], mean_var[s][:, t, 0:1],
                                               rstd[s][:, t:t + 1], ALU.subtract, ALU.mult)
                    last.then_inc(hn_made[s], 1)

                def layernorm(layer):
                    for s in SLOTS:
                        statistics(s, layer)
                    for s in SLOTS:
                        normalise(s, layer)

                def scores(s, call, mask):
                    before, heads = CALLS[call]
                    for h in range(heads):
                        held_until(dve, dve_passed, bcast[s], 7 * it + before + min(heads, h // 2 * 2 + 2))
                        row = halves(s, 0 if h < 2 else 3)[:, h % 2, :]
                        for t in range(T):
                            last = v.tensor_tensor_reduce(out=z[s][:, h, t, :], in0=row, in1=mask[:, t, :], scale=1.0,
                                                          scalar=LOWEST, op0=ALU.add, op1=ALU.max,
                                                          accum_out=row_max[s][:, t, h:h + 1])
                    last.then_inc(z_made[s], 1)
                    dve.wait_ge(z_made[s], 4 * it + call + 1)
                    v.tensor_tensor(row_top[s][:, :, 0:heads], row_max[s][:, :, 0:heads], cols[s][:, :, 0:heads, 1],
                                    ALU.add).then_inc(top_made[s], 1)
                    dve.wait_ge(top_made[s], 4 * it + call + 1)
                    v.tensor_scalar(row_low[s][:, :, 0:heads], row_top[s][:, :, 0:heads], -SLOPE, None,
                                    ALU.mult).then_inc(low_made[s], 1)
                    dve.wait_ge(low_made[s], 4 * it + call + 1)
                    v.scalar_tensor_tensor(neg_max[s][:, :, 0:heads], row_top[s][:, :, 0:heads], -1.0,
                                           row_low[s][:, :, 0:heads], ALU.mult, ALU.min).then_inc(neg_made[s], 1)

                def leaky(s, call):
                    before, heads = CALLS[call]
                    for h in range(heads):
                        dve.wait_ge(scaled[s], 7 * it + before + h + 1)
                        for t in range(T):
                            last = v.scalar_tensor_tensor(z[s][:, h, t, :], z[s][:, h, t, :], cols[s][:, t, h, 1:2],
                                                          pT[s][:, h, t, :], ALU.add, ALU.max)
                        last.then_inc(leaky_done[s], 1)

                def inverse_sums(s, call):
                    before, heads = CALLS[call]
                    dve.wait_ge(exp_done[s], 7 * it + before + heads)
                    v.reciprocal(rec[s][:, :, 0:heads], row_sum[s][:, :, 0:heads]).then_inc(rec_made[s], 1)
                    dve.wait_ge(rec_made[s], 5 * it + REC_OF[call])

                def take_pT(s, n, b, to):
                    if n not in BY_ACT:
                        dve.wait_ge(pT_psum[s], 14 * it + n + 1)
                        v.tensor_copy(pT[s][:, to, :, :], halves(s, b)).then_inc(pT_by_dve[s], 1)

                layernorm(0)
                for s in SLOTS:
                    dve.wait_ge(proj[s], 3 * it + 1)
                    v.tensor_copy(cols[s][:, :, 0, :], ps[s][:, 1:3, D:D + 2]).then_inc(cols_made[s], 1)
                for s in SLOTS:
                    held_until(dve, dve_passed, mask_t_made[s], it + 1)
                    scores(s, 0, mask_t[s])
                for s in SLOTS:
                    leaky(s, 0)
                for s in SLOTS:
                    inverse_sums(s, 0)
                    for t in range(T):
                        last = v.tensor_scalar(val[s][:, t, 0:D], bank(s, 1 + t)[:, 0:D], rec[s][:, t, 0:1], None,
                                               ALU.mult)
                    last.then_inc(val_made[s], 1)
                for s in SLOTS:
                    dve.wait_ge(low0[s], it + 1)
                    v.scalar_tensor_tensor(u[s][:, :, 0:D], halves(s, 3), 1.0, u[s][:, :, 0:D], ALU.mult,
                                           ALU.max).then_inc(leaky0[s], 1)
                for s in SLOTS:
                    dve.wait_ge(leaky0[s], it + 1)
                    v.tensor_tensor(x_run[s][:], x_in[s][:], u[s][:, :, 0:D], ALU.add).then_inc(x_made[s], 1)

                layernorm(1)
                for s in SLOTS:
                    dve.wait_ge(k_psum[s], it + 1)
                    v.tensor_copy(kT[s][:], halves(s, 2)).then_inc(k_made[s], 1)

                def max1(s, h):
                    dve.wait_ge(s_psum[s], 8 * it + h + 1)
                    v.tensor_reduce(neg_max1[s][:, h, :], halves(s, h % 2), AX.X, ALU.max,
                                    negate=True).then_inc(neg1_made[s], 1)

                for h in (0, 1):
                    for s in SLOTS:
                        max1(s, h)
                for h in range(HEADS1):
                    for s in SLOTS:
                        take_pT(s, h, 2, h % 4)
                        if h + 2 < HEADS1:
                            max1(s, h + 2)
                    if h == HEADS1 - 3:
                        continue
                for s in SLOTS:
                    dve.wait_ge(exp1_done[s], 8 * it + HEADS1)
                    v.reciprocal(rec1[s][:].rearrange("p t h d -> p (t h) d"),
                                 row_sum1[s][:].rearrange("p t h -> p (t h)").unsqueeze(2).to_broadcast(
                                     [P, T * HEADS1, DK])).then_inc(rec_made[s], 1)
                for s in SLOTS:
                    dve.wait_ge(o_psum[s], it + 1)
                    dve.wait_ge(r_made[s], it + 1)
                    v.scalar_tensor_tensor(oT[s][:], halves(s, 3), 0.0, rec_bc[s][:], ALU.max,
                                           ALU.mult).then_inc(oT_made[s], 1)
                for s in SLOTS:
                    dve.wait_ge(wo_psum[s], it + 1)
                    v.tensor_tensor(x_run[s][:], x_run[s][:], halves(s, 1), ALU.add).then_inc(x_made[s], 1)

                layernorm(2)
                for s in SLOTS:
                    dve.wait_ge(proj[s], 3 * it + 2)
                    v.tensor_copy(cols[s][:], bank(s, 3)[:, 0:T * HEADS2 * 2].rearrange(
                        "p (t h v) -> p t h v", t=T, v=2)).then_inc(cols_made[s], 1)
                    v.tensor_tensor(val[s][:], ps[s][:, 1:3, :], b1_bc[:].unsqueeze(1).to_broadcast([P, T, FH]),
                                    ALU.add).then_inc(val_made[s], 1)
                for s in SLOTS:
                    dve.wait_ge(mask_t_diag[s], it + 1)
                    scores(s, 1, mask_t[s])
                for s in SLOTS:
                    leaky(s, 1)
                for h in range(HEADS2):
                    for s in SLOTS:
                        take_pT(s, HEADS1 + h, (0, 3)[h % 2], h)
                for s in SLOTS:
                    inverse_sums(s, 1)
                    dve.wait_ge(pv2[s], it + 1)
                    v.tensor_tensor(u[s][:].rearrange("p t (h f) -> p (t h) f", h=HEADS2),
                                    ps[s][:, 1:3, :].rearrange("p t (h f) -> p (t h) f", h=HEADS2),
                                    rec[s][:].rearrange("p t h -> p (t h)").unsqueeze(2).to_broadcast(
                                        [P, T * HEADS2, F2]), ALU.mult).then_inc(u_made[s], 1)
                for s in SLOTS:
                    dve.wait_ge(e_made[s], it + 1)
                    v.scalar_tensor_tensor(u[s][:], e[s][:], 1.0, u[s][:], ALU.min, ALU.max).then_inc(h1_made[s], 1)
                for s in SLOTS:
                    dve.wait_ge(proj[s], 3 * it + 3)
                    v.tensor_copy(cols[s][:, :, 0, :], ps[s][:, 1:3, D:D + 2]).then_inc(cols_made[s], 1)
                    v.tensor_tensor(val[s][:, :, 0:D], ps[s][:, 1:3, 0:D],
                                    b2_bc[:].unsqueeze(1).to_broadcast([P, T, D]), ALU.add).then_inc(val_made[s], 1)
                for s in SLOTS:
                    scores(s, 2, mask_t[s])
                for s in SLOTS:
                    leaky(s, 2)
                for s in SLOTS:
                    take_pT(s, HEADS1 + HEADS2, 3, 0)

                def add_weighted(s, call, to):
                    inverse_sums(s, call)
                    dve.wait_ge(pv[s], 3 * it + call)
                    for t in range(T):
                        last = v.scalar_tensor_tensor(to[:, t, :], halves(s, 1)[:, t, :], rec[s][:, t, 0:1],
                                                      x_run[s][:, t, :], ALU.mult, ALU.add)
                    return last

                for s in SLOTS:
                    add_weighted(s, 2, x_run[s]).then_inc(x_made[s], 1)

                for s in SLOTS:
                    statistics(s, 3)
                for s in SLOTS:
                    normalise(s, 3)
                    dve.wait_ge(hn_made[s], 4 * it + 4)
                    v.tensor_scalar(hn[s][:], hn[s][:], 0.0, None, ALU.max).then_inc(relu3[s], 1)
                for s in SLOTS:
                    dve.wait_ge(relu3[s], it + 1)
                    for t in range(T):
                        for c in range(2):
                            last = v.tensor_tensor_reduce(out=e[s][:, t, c * D:(c + 1) * D], in0=hn[s][:, t, :], in1=w3_bc[:, c, :],
                                                          scale=1.0, scalar=0.0, op0=ALU.mult, op1=ALU.add,
                                                          accum_out=cols[s][:, t, 0, c:c + 1])
                    last.then_inc(raw3[s], 1)
                for s in SLOTS:
                    dve.wait_ge(raw3[s], it + 1)
                    v.tensor_scalar(cols[s][:, :, 0, 1], cols[s][:, :, 0, 1], b3_bc[:], None,
                                    ALU.add).then_inc(cols_made[s], 1)
                for s in SLOTS:
                    dve.wait_ge(mask_n_diag[s], it + 1)
                    scores(s, 3, mask_n[s])
                for s in SLOTS:
                    leaky(s, 3)
                for s in SLOTS:
                    take_pT(s, HEADS1 + HEADS2 + 1, 3, 0)
                for s in SLOTS:
                    dve.wait_ge(stored[s], 16 * it + 16)
                    add_weighted(s, 3, x_out[s]).then_inc(out_made[s], 1)


_INS = ['x', 'adj', 'L0_gnn_W', 'L0_gnn_a', 'L1_gnn_Wq', 'L1_gnn_Wk', 'L1_gnn_Wv', 'L1_gnn_Wo', 'L2_gnn_W1',
        'L2_gnn_att_src1', 'L2_gnn_att_dst1', 'L2_gnn_b1', 'L2_gnn_W2', 'L2_gnn_att_src2', 'L2_gnn_att_dst2',
        'L2_gnn_b2', 'L3_gnn_attn_w_src', 'L3_gnn_attn_w_dst', 'L3_gnn_attn_b']


def kernel(**inputs):
    import numpy as _np
    import concourse.bacc as _bacc
    from concourse import mybir as _mybir
    from concourse.bass_utils import run_bass_kernel_spmd as _run

    nc = _bacc.Bacc("TRN2", target_bir_lowering=False, num_devices=1)
    arrays, args = {}, []
    for name in _INS:
        a = _np.ascontiguousarray(inputs[name])
        arrays[f"in_{name}"] = a
        args.append(nc.dram_tensor(f"in_{name}", a.shape, _mybir.dt.from_np(a.dtype), kind="ExternalInput").ap())
    shape = arrays["in_x"].shape
    args.append(nc.dram_tensor("out_0", shape, _mybir.dt.float32, kind="ExternalOutput").ap())
    four_graph_layers(nc, *args)
    r = _run(nc, [arrays], core_ids=[0])
    return r.results[0]["out_0"]
```

```python
import concourse.bass as bass
from concourse import mybir
from contextlib import ExitStack


def four_graph_layers(nc, x, adj, w0, a0, wq, wk, wv, wo, w1, att_src1, att_dst1, b1, w2, att_src2,
                      att_dst2, b2, w_src3, w_dst3, b3, out):
    fp32, bf16, i32 = mybir.dt.float32, mybir.dt.bfloat16, mybir.dt.int32
    ALU, ACT, AX = mybir.AluOpType, mybir.ActivationFunctionType, mybir.AxisListType

    P = 128
    G, N, D = x.shape
    T = N // P
    C = D // P
    SLOTS = range(4)
    ROUNDS = G // len(SLOTS)
    HEADS1 = 8
    DK = D // HEADS1
    PER = P // DK
    HEADS2 = att_src1.shape[0]
    F2 = att_src1.shape[1]
    FH = HEADS2 * F2
    CH = FH // P
    SLOPE = 0.2
    EPS = 1e-5
    MASKED = -float(2 ** 53)
    LOWEST = -3.0e38
    ONE = D + 2

    with ExitStack() as ctx:
        def sb(name, shape, dt=fp32):
            return ctx.enter_context(nc.sbuf_tensor(name, shape, dt))

        def per_slot(name, shape, dt=fp32):
            return [sb(f"{name}_{s}", shape, dt) for s in SLOTS]

        def sem(name):
            return ctx.enter_context(nc.semaphore(name))

        def sems(name):
            return [sem(f"{name}_{s}") for s in SLOTS]

        ident = sb("ident", [P, P])
        ident16 = sb("ident16", [P, P], bf16)
        w0_sb = sb("w0_sb", [P, C, ONE])
        wq_sb, wk_sb, wv_sb, wo_sb = (sb(n, [P, C, D]) for n in ("wq_sb", "wk_sb", "wv_sb", "wo_sb"))
        w1_sb = sb("w1_sb", [P, C, FH])
        w1_cols = sb("w1_cols", [P, C, HEADS2, 2])
        w2_sb = sb("w2_sb", [P, CH, ONE])
        a0_sb = sb("a0_sb", [P, C, 2])
        att1_sb = sb("att1_sb", [P, HEADS2, 2])
        att2_sb = sb("att2_sb", [P, C, 2])
        b1_bc = sb("b1_bc", [P, FH])
        b2_bc = sb("b2_bc", [P, D])
        w3_bc = sb("w3_bc", [P, 2, D])
        b3_bc = sb("b3_bc", [P, 1])
        minus_one = sb("minus_one", [P, 1])
        minus_half = sb("minus_half", [P, T])

        adj_in = per_slot("adj_in", [P, T, N], i32)
        x_in = per_slot("x_in", [P, T, D])
        x_run = per_slot("x_run", [P, T, D])
        bn = per_slot("bn", [P, T, 6])
        mean_var = per_slot("mean_var", [P, T, 2])
        var_eps = per_slot("var_eps", [P, T])
        rstd = per_slot("rstd", [P, T])
        hn = per_slot("hn", [P, T, D])
        hT = per_slot("hT", [P, C, N])
        mask_n = per_slot("mask_n", [P, T, N], bf16)
        mask_t = per_slot("mask_t", [P, T, N], bf16)
        val = per_slot("val", [P, T, FH])
        cols = per_slot("cols", [P, T, HEADS2, 2])
        z = per_slot("z", [P, 4, T, N])
        row_max = per_slot("row_max", [P, T, HEADS2])
        row_top = per_slot("row_top", [P, T, HEADS2])
        row_low = per_slot("row_low", [P, T, HEADS2])
        neg_max = per_slot("neg_max", [P, T, HEADS2])
        neg_max1 = per_slot("neg_max1", [P, HEADS1, T])
        row_sum = per_slot("row_sum", [P, T, HEADS2])
        rec = per_slot("rec", [P, T, HEADS2])
        row_sum1 = per_slot("row_sum1", [P, T, HEADS1])
        inv1 = per_slot("inv1", [P, T, HEADS1])
        pT = per_slot("pT", [P, 4, T, N])
        wide = per_slot("wide", [P, 2, T, FH])

        u = [w[:, 0] for w in wide]
        e = [w[:, 1] for w in wide]
        kT = [w[:].rearrange("p a t (b n) -> p (a t b) n", n=N) for w in wide]
        rec1 = [w[:, 0].rearrange("p t f -> p (t f)")[:, 0:T * D].rearrange("p (t h d) -> p t h d", t=T, h=HEADS1)
                for w in wide]
        qT = hn
        oT = hT
        h1T = [m[:, 2:4].rearrange("p h t n -> p (h t) n") for m in z]
        wT_sb = z[0][:, 0:2].rearrange("p h t n -> p h (t n)")

        ps = [ctx.enter_context(nc.psum_tensor(f"ps_{s}", [P, 2, 512], fp32)) for s in SLOTS]

        def bank(s, b):
            return ps[s][:, b, :]

        def col(s, call, t, h, v):
            return val[s][:, t, D + v:D + v + 1] if call in (0, 2) else cols[s][:, t, h, v:v + 1]

        def halves(s, b):
            return ps[s][:, b, :].rearrange("p (t n) -> p t n", t=2)

        consts_in = sem("consts_in")
        ident_made = sem("ident_made")
        setup_psum, setup_sb = sem("setup_psum"), sem("setup_sb")
        setup_done = sem("setup_done")
        loaded, stored = sems("loaded"), sems("stored")
        MASKS = ("mask_n", "mask_t diagonal", "mask_n diagonal")
        masks = sems("masks")
        PREPARED = ("keys cleared", "val + b1", "x + b2")
        prepared = sems("prepared")
        TURNED = ("mask_t", "hT 0", "hT 1", "hT 2", "h1T 0", "h1T 1")
        turned, turned_taken = sems("turned"), sems("turned_taken")
        PROJECTED = ("layer 0", "q", "k", "v", "1 / sums", "wo", "terms 2", "xl 0", "xl 1", "layer 2b")
        projected = sems("projected")
        SUMMED = ("layer 0", "layer 1 heads 0", "layer 1 heads 1", "layer 2a tile 0", "layer 2a tile 1",
                  "layer 2b", "layer 3")
        summed = sems("summed")
        OUTPUTS = ("slope * layer 0", "layer 1 heads 0", "layer 1 heads 1")
        outputs_taken = sems("outputs_taken")
        DVE_STEPS = ("scaled val", "leaky 0", "k", "1 / sums", "oT", "relu 3", "raw terms 3")
        dve_steps = sems("dve_steps")
        X_MADE = ("free", "layer 0", "layer 1", "layer 2")
        x_made = sems("x_made")
        stat_steps = sems("stat_steps")
        rstd_steps, hn_made = sems("rstd_steps"), sems("hn_made")
        cols_made, val_made = sems("cols_made"), sems("val_made")
        bcast = sems("bcast")
        max_steps = sems("max_steps")
        scaled, leaky_done, exp_done = sems("scaled"), sems("leaky_done"), sems("exp_done")
        rec_made = sems("rec_made")
        pT_psum = sems("pT_psum")
        pT_by_act, pT_by_dve = sems("pT_by_act"), sems("pT_by_dve")
        qv_made = sems("qv_made")
        s_psum, neg1_made, exp1_done = sems("s_psum"), sems("neg1_made"), sems("exp1_done")
        e_made, h1_steps = sems("e_made"), sems("h1_steps")
        dve_passed, pool_passed = sem("dve_passed"), sem("pool_passed")

        def value(steps, it, step):
            return len(steps) * it + steps.index(step) + 1

        BY_ACT = {1, 3, 5, 7, 9, 11}
        CALLS = ((0, 1), (1, HEADS2), (1 + HEADS2, 1), (2 + HEADS2, 1))
        UNITS = ((0, 0, 1), (1, 0, 2), (1, 2, 2), (2, 0, 1), (3, 0, 1))
        PT_OF = (None, HEADS1, HEADS1 + HEADS2, HEADS1 + HEADS2 + 1)
        REC_OF = (1, 3, 4, 5)

        ALL_PT = HEADS1 + HEADS2 + 2

        def wait_pT(eng, s, it, n):
            by_act = len([m for m in BY_ACT if m <= n])
            if by_act:
                eng.wait_ge(pT_by_act[s], len(BY_ACT) * it + by_act)
            if n + 1 - by_act:
                eng.wait_ge(pT_by_dve[s], (ALL_PT - len(BY_ACT)) * it + n + 1 - by_act)

        def held_until(eng, passed, semaphore, value):
            eng.wait_ge(semaphore, value)
            eng.sem_inc(passed, 1)

        x_v = x.rearrange("g (t p) d -> g p t d", p=P)
        adj_v = adj.rearrange("g (t p) n -> g p t n", p=P)
        out_v = out.rearrange("g (t p) d -> g p t d", p=P)


        LENGTH, BEHIND = 85, (0, 3, 6, 9)
        TIMES = {
            "PE": [(2, "mask_t", 0), (4, "hT", 0), (5, "proj0", 0), (6, "row", 0), (12, "out0", 0), (17, "hT", 1),
                    (18, "qkv", 0), (19, "v", 0), (20, "scores1", 0), (21, "scores1", 1), (22, "turn1", 0),
                    (23, "scores1", 2), (24, "turn1", 1), (25, "scores1", 3), (26, "turn1", 2), (27, "scores1", 4),
                    (28, "turn1", 3), (29, "sum1", 0), (30, "scores1", 5), (31, "turn1", 4), (32, "scores1", 6),
                    (33, "turn1", 5), (34, "scores1", 7), (35, "turn1", 6), (36, "turn1", 7), (37, "sum1", 1),
                    (40, "rows1", 0), (42, "wo", 0), (45, "hT", 2), (46, "proj2", 0), (47, "row", 1), (48, "row", 2),
                    (49, "xl", 0), (57, "turn2", 0), (58, "turn2", 1), (59, "turn2", 2), (60, "turn2", 3),
                    (61, "sum2", 0), (66, "h1T", 0), (67, "proj3", 0), (68, "row", 3), (72, "turn3", 0),
                    (73, "out3", 0), (78, "row", 4), (82, "turn4", 0), (83, "out4", 0)],
            "DVE": [(1, "stats", 0), (3, "norm", 0), (6.1, "row", 0), (9, "leaky", 0), (11, "sum0", 0),
                    (13, "add0", 0), (15, "stats", 1), (16, "norm", 1), (18.2, "qkv", 0), (20.1, "scores1", 0),
                    (21.1, "scores1", 1), (22.1, "turn1", 0), (23.1, "scores1", 2), (25.1, "scores1", 3),
                    (26.1, "turn1", 2), (27.1, "scores1", 4), (30.1, "scores1", 5), (31.1, "turn1", 4),
                    (32.1, "scores1", 6), (34.1, "scores1", 7), (35.1, "turn1", 6), (38, "rec1", 0), (41, "oT", 0),
                    (42.1, "wo", 0), (43, "stats", 2), (44, "norm", 2), (46.1, "proj2", 0), (47.1, "row", 1),
                    (48.1, "row", 2), (53, "leaky", 1), (55, "leaky", 2), (57.1, "turn2", 0), (59.1, "turn2", 2),
                    (62, "rec2", 0), (63, "u", 0), (65, "elu", 0), (68.1, "row", 3), (70, "leaky", 3),
                    (72.1, "turn3", 0), (74, "add3", 0), (75, "stats", 3), (76, "norm", 3), (77, "cols4", 0),
                    (78.1, "row", 4), (80, "leaky", 4), (82.1, "turn4", 0), (84, "add4", 0)],
            "ACT": [(2.1, "mask_t", 0), (4.1, "hT", 0), (5.1, "proj0", 0), (10, "exp", 0), (12.1, "out0", 0),
                    (17.1, "hT", 1), (18.1, "qkv", 0), (19.1, "v", 0), (20.2, "scores1", 0), (21.2, "scores1", 1),
                    (23.2, "scores1", 2), (24.1, "turn1", 1), (25.2, "scores1", 3), (27.2, "scores1", 4),
                    (28.1, "turn1", 3), (29.1, "sum1", 0), (30.2, "scores1", 5), (32.2, "scores1", 6),
                    (33.1, "turn1", 5), (34.2, "scores1", 7), (36.1, "turn1", 7), (37.1, "sum1", 1), (45.1, "hT", 2),
                    (49.1, "xl", 0), (54, "exp", 1), (56, "exp", 2), (58.1, "turn2", 1), (60.1, "turn2", 3),
                    (64, "exp_u", 0), (66.1, "h1T", 0), (67.1, "proj3", 0), (71, "exp", 3), (81, "exp", 4)],
            "Pool": [(0, "masks", 0), (1.1, "stats", 0), (7, "scale", 0), (8, "diag_t", 0), (14, "clear", 0),
                    (15.1, "stats", 1), (39, "diag_n", 0), (43.1, "stats", 2), (49.2, "xl", 0), (50, "bias2", 0),
                    (51, "scale", 1), (52, "scale", 2), (69, "scale", 3), (75.1, "stats", 3), (79, "scale", 4)],
        }

        def walk(eng, who, stage):
            def turn(it, rounds):
                order = []
                for s in SLOTS:
                    for tau, name, n in TIMES[who]:
                        back = 1 if tau + BEHIND[s] >= LENGTH else 0
                        if back in rounds:
                            order.append((tau + BEHIND[s] - back * LENGTH, s, back, name, n))
                order.sort()
                for _, s, back, name, n in order:
                    stage(s, it - back if back else it, name, n)

            if max(tau for tau, name, n in TIMES[who]) + max(BEHIND) >= LENGTH:
                turn(0, (0,))
                with eng.Fori(1, ROUNDS) as it:
                    turn(it, (0, 1))
                turn(ROUNDS, (1,))
            else:
                with eng.Fori(0, ROUNDS) as it:
                    turn(it, (0,))

        block = ctx.enter_context(nc.Block())

        @block.sync
        def _(sp):
            for dst, src in ((w0_sb[:, :, 0:D], w0), (wq_sb[:], wq), (wk_sb[:], wk), (wv_sb[:], wv),
                             (wo_sb[:], wo), (w1_sb[:], w1), (w2_sb[:, :, 0:D], w2)):
                sp.dma_start(dst, src.rearrange("(c p) n -> p c n", p=P)).then_inc(consts_in, 16)
            with nc.allow_non_contiguous_dma(reason="vectors laid along the partitions, once"):
                for half in range(2):
                    sp.dma_start(a0_sb[:, :, half],
                                 a0[half * D:(half + 1) * D, 0].rearrange("(c p) -> p c", p=P)).then_inc(consts_in, 16)
                sp.dma_start(att1_sb[:, :, 0], att_src1.rearrange("h f -> f h")).then_inc(consts_in, 16)
                sp.dma_start(att1_sb[:, :, 1], att_dst1.rearrange("h f -> f h")).then_inc(consts_in, 16)
                sp.dma_start(att2_sb[:, :, 0], att_src2.rearrange("o (c p) -> p (o c)", p=P)).then_inc(consts_in, 16)
                sp.dma_start(att2_sb[:, :, 1], att_dst2.rearrange("o (c p) -> p (o c)", p=P)).then_inc(consts_in, 16)
            for dst, src in ((b1_bc[:], b1), (b2_bc[:], b2), (w3_bc[:, 0, :], w_dst3), (w3_bc[:, 1, :], w_src3),
                             (b3_bc[:], b3)):
                sp.dma_start(dst, src.partition_broadcast(P)).then_inc(consts_in, 16)

            def load(g, s):
                sp.dma_start(adj_in[s][:], adj_v[bass.ds(g, 1)].squeeze(0) if not isinstance(g, int) else adj_v[g]).then_inc(loaded[s], 16)
                sp.dma_start(x_in[s][:], x_v[bass.ds(g, 1)].squeeze(0) if not isinstance(g, int) else x_v[g]).then_inc(loaded[s], 16)

            def store(g, s):
                sp.dma_start(out_v[bass.ds(g, 1)].squeeze(0) if not isinstance(g, int) else out_v[g], x_run[s][:]).then_inc(stored[s], 16)

            for s in SLOTS:
                sp.sem_inc(stored[s], 16)
                sp.sem_inc(x_made[s], 1)
                load(s, s)
            with sp.Fori(0, ROUNDS - 1) as it:
                for s in SLOTS:
                    sp.wait_ge(masks[s], value(MASKS, it, "mask_n"))
                    sp.wait_ge(x_made[s], value(X_MADE, it, "layer 0"))
                    load(len(SLOTS) * it + (len(SLOTS) + s), s)
                for s in SLOTS:
                    sp.wait_ge(x_made[s], value(X_MADE, it, "free") + len(X_MADE))
                    store(len(SLOTS) * it + s, s)
            for s in SLOTS:
                sp.wait_ge(x_made[s], value(X_MADE, ROUNDS, "free"))
                store(G - len(SLOTS) + s, s)
            for s in SLOTS:
                sp.wait_ge(stored[s], 16 * (ROUNDS + 1))

        @block.gpsimd
        def _(pool):
            nc.gpsimd.memset(ident[:], 0.0).then_inc(ident_made, 1)
            nc.gpsimd.memset(minus_one[:], -1.0)
            nc.gpsimd.memset(minus_half[:], -0.5)
            pool.wait_ge(ident_made, 1)
            nc.gpsimd.affine_select(out=ident[:], in_=ident[:], compare_op=ALU.not_equal, fill=1.0, base=0,
                                    pattern=[[-1, P]], channel_multiplier=1).then_inc(ident_made, 1)
            pool.wait_ge(ident_made, 2)
            nc.gpsimd.tensor_copy(ident16[:], ident[:]).then_inc(ident_made, 1)

            def inverse_std(s, it, layer):
                held_until(pool, pool_passed, stat_steps[s], 16 * it + 4 * layer + 4)
                nc.gpsimd.tensor_scalar(var_eps[s][:], mean_var[s][:, :, 1], EPS, 1.0, ALU.add,
                                        ALU.mult).then_inc(rstd_steps[s], 1)
                pool.wait_ge(rstd_steps[s], 8 * it + 2 * layer + 1)
                nc.gpsimd.tensor_tensor(rstd[s][:], var_eps[s][:], minus_half[:], ALU.pow).then_inc(rstd_steps[s], 1)

            def open_diagonal(s, mask):
                for t in range(T):
                    v = mask[:, t, t * P:(t + 1) * P]
                    last = nc.gpsimd.affine_select(out=v, in_=v, compare_op=ALU.not_equal, fill=0.0, base=0,
                                                   pattern=[[-1, P]], channel_multiplier=1)
                last.then_inc(masks[s], 1)

            def scale_scores(s, it, unit):
                call, first, heads = UNITS[unit]
                held_until(pool, pool_passed, max_steps[s], 4 * (5 * it + unit) + 1)
                for h in range(first, first + heads):
                    for t in range(T):
                        last = nc.gpsimd.tensor_scalar(pT[s][:, h, t, :], z[s][:, h, t, :],
                                                       col(s, call, t, h, 1), SLOPE, ALU.add, ALU.mult)
                    last.then_inc(scaled[s], 1)

            def stage(s, it, name, n):
                if name == "masks":
                    held_until(pool, pool_passed, x_made[s], value(X_MADE, it, "free"))
                    held_until(pool, pool_passed, loaded[s], 32 * it + 32)
                    nc.gpsimd.tensor_scalar(mask_n[s][:], adj_in[s][:], 0, MASKED, ALU.is_le,
                                            ALU.mult).then_inc(masks[s], 1)
                elif name == "stats":
                    inverse_std(s, it, n)
                elif name == "scale":
                    scale_scores(s, it, n)
                elif name == "clear":
                    held_until(pool, pool_passed, x_made[s], value(X_MADE, it, "layer 0"))
                    nc.gpsimd.memset(wide[s][:], 0.0).then_inc(prepared[s], 1)
                elif name == "xl":
                    pool.wait_ge(val_made[s], 4 * it + 3)
                    nc.gpsimd.tensor_tensor(val[s][:], val[s][:], b1_bc[:].unsqueeze(1).to_broadcast([P, T, FH]),
                                            ALU.add).then_inc(prepared[s], 1)
                elif name == "bias2":
                    pool.wait_ge(hn_made[s], 4 * it + 3)
                    nc.gpsimd.tensor_tensor(x_run[s][:], x_run[s][:], b2_bc[:].unsqueeze(1).to_broadcast([P, T, D]),
                                            ALU.add).then_inc(prepared[s], 1)
                elif name == "diag_t":
                    open_diagonal(s, mask_t[s])
                elif name == "diag_n":
                    held_until(pool, pool_passed, s_psum[s], 8 * it + HEADS1)
                    open_diagonal(s, mask_n[s])

            walk(pool, "Pool", stage)

        @block.tensor
        def _(pe):
            mm, tr = nc.tensor.matmul, nc.tensor.transpose

            pe.wait_ge(consts_in, 16 * 18)
            pe.wait_ge(ident_made, 3)
            for f in range(C):
                for c in range(C):
                    last = tr(bank(0, f)[:, c * P:(c + 1) * P], w0_sb[:, c, f * P:(f + 1) * P], ident[:])
            last.then_inc(setup_psum, 1)
            pe.wait_ge(setup_sb, 1)
            for c in range(C):
                for f in range(C):
                    last = mm(bank(1, 0)[:, 2 * c:2 * c + 2], wT_sb[:, f, c * P:(c + 1) * P], a0_sb[:, f, :],
                              start=(f == 0), stop=(f == C - 1))
            last.then_inc(setup_psum, 1)
            for h in range(HEADS2):
                pe.wait_ge(setup_sb, 2 + h)
                for c in range(C):
                    last = tr(bank(0, 0)[:, c * P:(c + 1) * P], w1_sb[:, c, h * F2:(h + 1) * F2], ident[:])
                last.then_inc(setup_psum, 1)
                pe.wait_ge(setup_sb, 3 + h)
                for c in range(C):
                    last = mm(bank(1, 1)[:, (c * HEADS2 + h) * 2:(c * HEADS2 + h) * 2 + 2],
                              wT_sb[:, 0, c * P:(c + 1) * P], att1_sb[:, h, :], start=True, stop=True)
            last.then_inc(setup_psum, 1)
            for f in range(C):
                for c in range(CH):
                    last = tr(bank(2, f)[:, c * P:(c + 1) * P], w2_sb[:, c, f * P:(f + 1) * P], ident[:])
            last.then_inc(setup_psum, 1)
            pe.wait_ge(setup_sb, 4 + HEADS2)
            for c in range(CH):
                for f in range(C):
                    last = mm(bank(1, 0)[:, 2 * c:2 * c + 2], wT_sb[:, f, c * P:(c + 1) * P], att2_sb[:, f, :],
                              start=(f == 0), stop=(f == C - 1))
            last.then_inc(setup_psum, 1)
            pe.wait_ge(setup_done, 1)

            def transpose_h(s, it, layer):
                pe.wait_ge(hn_made[s], 4 * it + layer + 1)
                for c in range(C):
                    for t in range(T):
                        last = tr(halves(s, 0)[:, c, t * P:(t + 1) * P], hn[s][:, t, c * P:(c + 1) * P], ident[:])
                last.then_inc(turned[s], 1)

            def project(s, left, n_in, w, width):
                for t in range(T):
                    for c in range(n_in):
                        last = mm(bank(s, t)[:, 0:width], left[:, c, t * P:(t + 1) * P], w[:, c, :],
                                  start=(c == 0), stop=(c == n_in - 1))
                return last

            def broadcast_scores(s, it, unit):
                call, first, heads = UNITS[unit]
                if call in (0, 2):
                    pe.wait_ge(val_made[s], 4 * it + (1, None, 4)[call])
                else:
                    pe.wait_ge(cols_made[s], 2 * it + (1 if call == 1 else 2))
                for h in range(first, first + heads):
                    to = halves(s, 0 if h < 2 else 1)[:, h % 2, :]
                    for t in range(T):
                        last = tr(to[:, t * P:(t + 1) * P], col(s, call, t, h, 0).to_broadcast([P, P]), ident[:])
                last.then_inc(bcast[s], 1)

            def transpose_p(s, b, h):
                for m in range(T):
                    for t in range(T):
                        last = tr(halves(s, b)[:, m, t * P:(t + 1) * P], z[s][:, h, t, m * P:(m + 1) * P], ident[:])
                last.then_inc(pT_psum[s], 1)

            def scores1(s, it, h):
                f = h // PER
                if h >= 2:
                    wait_pT(pe, s, it, h - 2)
                if h == PER + 1:
                    pe.wait_ge(outputs_taken[s], value(OUTPUTS, it, "layer 1 heads 0"))
                for t in range(T):
                    mm(halves(s, h % 2)[:, t, :], ident16[:], mask_n[s][:, t, :], start=True, stop=False)
                    last = mm(halves(s, h % 2)[:, t, :], qT[s][:, f, t * P:(t + 1) * P], kT[s][:, h, :],
                              start=False, stop=True)
                last.then_inc(s_psum[s], 1)

            def weighted(s, it, call, rows):
                wait_pT(pe, s, it, PT_OF[call])
                for d in range(T):
                    for m in range(T):
                        last = mm(halves(s, 0)[:, d, :], pT[s][:, 0, m, d * P:(d + 1) * P], rows[:, m, 0:D],
                                  start=(m == 0), stop=(m == T - 1))
                last.then_inc(summed[s], 1)

            def stage(s, it, name, n):
                if name == "mask_t":
                    pe.wait_ge(masks[s], value(MASKS, it, "mask_n"))
                    to = bank(s, 1).bitcast(bf16)
                    for t in range(T):
                        for r in range(T):
                            last = tr(to[:, t * N + r * P:t * N + (r + 1) * P], mask_n[s][:, r, t * P:(t + 1) * P],
                                      ident16[:])
                    last.then_inc(turned[s], 1)
                elif name == "hT":
                    transpose_h(s, it, n)
                elif name == "proj0":
                    pe.wait_ge(turned_taken[s], value(TURNED, it, "hT 0"))
                    pe.wait_ge(turned_taken[s], value(TURNED, it, "mask_t"))
                    project(s, hT[s], C, w0_sb, ONE).then_inc(projected[s], 1)
                elif name == "row":
                    broadcast_scores(s, it, n)
                elif name == "out0":
                    pe.wait_ge(exp_done[s], 7 * it + 1)
                    pe.wait_ge(dve_steps[s], value(DVE_STEPS, it, "scaled val"))
                    for i in range(T):
                        for j in range(T):
                            last = mm(halves(s, 0)[:, i, :], z[s][:, 0, j, i * P:(i + 1) * P], val[s][:, j, 0:D],
                                      start=(j == 0), stop=(j == T - 1))
                    last.then_inc(summed[s], 1)
                elif name == "qkv":
                    pe.wait_ge(turned_taken[s], value(TURNED, it, "hT 1"))
                    for w, b in ((wq_sb, 1), (wk_sb, 0)):
                        for f in range(C):
                            for c in range(C):
                                last = mm(halves(s, b)[:, f, :], w[:, c, f * P:(f + 1) * P], hT[s][:, c, :],
                                          start=(c == 0), stop=(c == C - 1))
                        last.then_inc(projected[s], 1)
                elif name == "v":
                    pe.wait_ge(qv_made[s], 2 * it + 1)
                    for t in range(T):
                        for c in range(C):
                            last = mm(halves(s, 1)[:, t, :], hT[s][:, c, t * P:(t + 1) * P], wv_sb[:, c, :],
                                      start=(c == 0), stop=(c == C - 1))
                    last.then_inc(projected[s], 1)
                elif name == "scores1":
                    if n == 0:
                        pe.wait_ge(dve_steps[s], value(DVE_STEPS, it, "k"))
                    if n == 1:
                        pe.wait_ge(qv_made[s], 2 * it + 2)
                    scores1(s, it, n)
                elif name == "turn1":
                    pe.wait_ge(exp1_done[s], 8 * it + n + 1)
                    transpose_p(s, n % 2, n % 4)
                elif name == "sum1":
                    wait_pT(pe, s, it, PER * (n + 1) - 1)
                    for m in range(T):
                        for j in range(PER):
                            h = PER * n + j
                            last = mm(halves(s, 1)[DK * j:DK * (j + 1), 0, :], val[s][:, m, h * DK:(h + 1) * DK],
                                      pT[s][:, j, m, :], start=(m == 0), stop=(m == T - 1))
                    last.then_inc(summed[s], 1)
                elif name == "rows1":
                    pe.wait_ge(rec_made[s], 5 * it + 2)
                    for f in range(C):
                        for t in range(T):
                            last = tr(halves(s, 0)[:, f, t * P:(t + 1) * P],
                                      rec1[s][:, t, PER * f:PER * (f + 1), :].rearrange("p h d -> p (h d)"), ident[:])
                    last.then_inc(projected[s], 1)
                elif name == "wo":
                    pe.wait_ge(dve_steps[s], value(DVE_STEPS, it, "oT"))
                    for t in range(T):
                        for c in range(C):
                            last = mm(halves(s, 1)[:, t, :], oT[s][:, c, t * P:(t + 1) * P], wo_sb[:, c, :],
                                      start=(c == 0), stop=(c == C - 1))
                    last.then_inc(projected[s], 1)
                elif name == "proj2":
                    pe.wait_ge(turned_taken[s], value(TURNED, it, "hT 2"))
                    for t in range(T):
                        for c in range(C):
                            last = mm(bank(s, 1)[:, t * 2 * HEADS2:(t + 1) * 2 * HEADS2],
                                      hT[s][:, c, t * P:(t + 1) * P], w1_cols[:, c, :, :].rearrange("p h v -> p (h v)"),
                                      start=(c == 0), stop=(c == C - 1))
                    last.then_inc(projected[s], 1)
                elif name == "xl":
                    for t in range(T):
                        pe.wait_ge(max_steps[s], 4 * (5 * it + t + 1) + 1)
                        for c in range(C):
                            last = mm(bank(s, t), hT[s][:, c, t * P:(t + 1) * P], w1_sb[:, c, :],
                                      start=(c == 0), stop=(c == C - 1))
                        last.then_inc(projected[s], 1)
                elif name == "turn2":
                    pe.wait_ge(exp_done[s], 7 * it + 2 + n)
                    if n < 2:
                        pe.wait_ge(val_made[s], 4 * it + 2 + n)
                    else:
                        wait_pT(pe, s, it, HEADS1 + n - 2)
                    transpose_p(s, n % 2, n)
                elif name == "sum2":
                    pe.wait_ge(prepared[s], value(PREPARED, it, "val + b1"))
                    wait_pT(pe, s, it, HEADS1 + HEADS2 - 1)
                    for d in range(T):
                        for h in range(HEADS2):
                            for m in range(T):
                                last = mm(bank(s, d)[:, h * F2:(h + 1) * F2], pT[s][:, h, m, d * P:(d + 1) * P],
                                          val[s][:, m, h * F2:(h + 1) * F2], start=(m == 0), stop=(m == T - 1))
                        last.then_inc(summed[s], 1)
                elif name == "h1T":
                    pe.wait_ge(h1_steps[s], 4 * it + 2 * T)
                    for half in range(2):
                        for c in range(CH // 2):
                            for t in range(T):
                                last = tr(halves(s, half)[:, c, t * P:(t + 1) * P],
                                          u[s][:, t, (CH // 2 * half + c) * P:(CH // 2 * half + c + 1) * P], ident[:])
                        last.then_inc(turned[s], 1)
                elif name == "proj3":
                    pe.wait_ge(turned_taken[s], value(TURNED, it, "h1T 1"))
                    project(s, h1T[s], CH, w2_sb, ONE).then_inc(projected[s], 1)
                elif name in ("turn3", "turn4"):
                    pe.wait_ge(exp_done[s], 7 * it + 3 + int(name[-1]))
                    transpose_p(s, 1, 0)
                elif name == "out3":
                    weighted(s, it, 2, val[s])
                elif name == "out4":
                    weighted(s, it, 3, hn[s])

            walk(pe, "PE", stage)

        @block.scalar
        def _(act):
            fn = nc.scalar.activation

            def softmax(s, it, unit):
                call, first, heads = UNITS[unit]
                act.wait_ge(max_steps[s], 4 * (5 * it + unit) + 4)
                for h in range(first, first + heads):
                    act.wait_ge(leaky_done[s], 7 * it + CALLS[call][0] + h + 1)
                    for t in range(T):
                        last = fn(z[s][:, h, t, :], z[s][:, h, t, :], ACT.Exp, bias=neg_max[s][:, t, h:h + 1],
                                  accum_out=row_sum[s][:, t, h:h + 1])
                    last.then_inc(exp_done[s], 1)

            def take_pT(s, it, n, b, to):
                if n in BY_ACT:
                    act.wait_ge(pT_psum[s], 14 * it + n + 1)
                    fn(pT[s][:, to, :, :], halves(s, b), ACT.Copy).then_inc(pT_by_act[s], 1)

            def exp1(s, it, h):
                act.wait_ge(neg1_made[s], 8 * it + h + 1)
                for t in range(T):
                    last = fn(z[s][:, h % 4, t, :], halves(s, h % 2)[:, t, :], ACT.Exp,
                              bias=neg_max1[s][:, h, t:t + 1], accum_out=row_sum1[s][:, t, h:h + 1])
                last.then_inc(exp1_done[s], 1)

            def stage(s, it, name, n):
                if name == "mask_t":
                    act.wait_ge(turned[s], value(TURNED, it, "mask_t"))
                    fn(mask_t[s][:].rearrange("p t n -> p (t n)"), bank(s, 1).bitcast(bf16)[:, 0:T * N],
                       ACT.Copy).then_inc(turned_taken[s], 1)
                elif name == "hT":
                    act.wait_ge(turned[s], value(TURNED, it, f"hT {n}"))
                    fn(hT[s][:], halves(s, 0), ACT.Relu).then_inc(turned_taken[s], 1)
                elif name == "exp":
                    softmax(s, it, n)
                elif name in ("proj0", "proj3"):
                    act.wait_ge(projected[s], value(PROJECTED, it, "layer 0" if name == "proj0" else "layer 2b"))
                    fn(val[s][:, :, 0:ONE], ps[s][:, :, 0:ONE], ACT.Copy).then_inc(val_made[s], 1)
                elif name == "xl":
                    for t in range(T):
                        act.wait_ge(projected[s], value(PROJECTED, it, f"xl {t}"))
                        fn(val[s][:, t, :], bank(s, t), ACT.Copy).then_inc(val_made[s], 1)
                elif name == "qkv":
                    act.wait_ge(projected[s], value(PROJECTED, it, "q"))
                    fn(qT[s][:], halves(s, 1), ACT.Copy, scale=float(DK) ** -0.5).then_inc(qv_made[s], 1)
                elif name == "v":
                    act.wait_ge(projected[s], value(PROJECTED, it, "v"))
                    fn(val[s][:, :, 0:D], halves(s, 1), ACT.Copy).then_inc(qv_made[s], 1)
                elif name == "scores1":
                    exp1(s, it, n)
                elif name == "turn1":
                    take_pT(s, it, n, n % 2, n % 4)
                elif name == "out0":
                    act.wait_ge(summed[s], value(SUMMED, it, "layer 0"))
                    fn(u[s][:, :, 0:D], halves(s, 0), ACT.Copy, scale=SLOPE).then_inc(outputs_taken[s], 1)
                elif name == "sum1":
                    act.wait_ge(summed[s], value(SUMMED, it, f"layer 1 heads {n}"))
                    fn(oT[s][:, n, :], halves(s, 1)[:, 0, :], ACT.Relu).then_inc(outputs_taken[s], 1)
                elif name == "turn2":
                    take_pT(s, it, HEADS1 + n, n % 2, n)
                elif name == "exp_u":
                    for t in range(T):
                        act.wait_ge(h1_steps[s], 4 * it + t + 1)
                        fn(e[s][:, t, :], u[s][:, t, :], ACT.Exp, bias=minus_one[:]).then_inc(e_made[s], 1)
                elif name == "h1T":
                    for half in range(2):
                        act.wait_ge(turned[s], value(TURNED, it, f"h1T {half}"))
                        fn(h1T[s][:, CH // 2 * half:CH // 2 * (half + 1), :], halves(s, half), ACT.Identity,
                           bias=minus_one[:]).then_inc(turned_taken[s], 1)
                elif name in ("turn3", "turn4"):
                    take_pT(s, it, PT_OF[int(name[-1]) - 1], 1, 0)

            walk(act, "ACT", stage)

        @block.vector
        def _(dve):
            v = nc.vector
            dve.wait_ge(setup_psum, 1)
            v.tensor_copy(wT_sb[:, :, 0:D], ps[0][:, 0:2, 0:D]).then_inc(setup_sb, 1)
            dve.wait_ge(setup_psum, 2)
            v.tensor_copy(w0_sb[:, :, D:D + 2],
                          bank(1, 0)[:, 0:2 * C].rearrange("p (c v) -> p c v", v=2)).then_inc(setup_sb, 1)
            for h in range(HEADS2):
                dve.wait_ge(setup_psum, 3 + h)
                v.tensor_copy(wT_sb[:, 0, 0:D], bank(0, 0)[:, 0:D]).then_inc(setup_sb, 1)
            dve.wait_ge(setup_psum, 3 + HEADS2)
            v.tensor_copy(w1_cols[:].rearrange("p c h v -> p (c h v)"),
                          bank(1, 1)[:, 0:C * HEADS2 * 2]).then_inc(setup_sb, 1)
            dve.wait_ge(setup_psum, 4 + HEADS2)
            v.tensor_copy(wT_sb[:, :, 0:FH], ps[2][:, :, 0:FH]).then_inc(setup_sb, 1)
            dve.wait_ge(consts_in, 16 * 18)
            v.tensor_scalar(b1_bc[:], b1_bc[:], 1.0, None, ALU.add)
            dve.wait_ge(setup_psum, 5 + HEADS2)
            v.tensor_copy(w2_sb[:, :, D:D + 2],
                          bank(1, 0)[:, 0:2 * CH].rearrange("p (c v) -> p c v", v=2)).then_inc(setup_done, 1)
            dve.wait_ge(setup_done, 1)

            def statistics(s, it, layer):
                src = x_run[s] if layer else x_in[s]
                if layer:
                    dve.wait_ge(x_made[s], value(X_MADE, it, f"layer {layer - 1}"))
                else:
                    dve.wait_ge(loaded[s], 32 * it + 32)
                for t in range(T):
                    v.bn_stats(bn[s][:, t, :], src[:, t, :]).then_inc(stat_steps[s], 1)
                for t in range(T):
                    held_until(dve, dve_passed, stat_steps[s], 16 * it + 4 * layer + t + 1)
                    v.bn_aggr(mean_var[s][:, t, :], bn[s][:, t, :]).then_inc(stat_steps[s], 1)

            def normalise(s, it, layer):
                src = x_run[s] if layer else x_in[s]
                dve.wait_ge(rstd_steps[s], 8 * it + 2 * layer + 2)
                for t in range(T):
                    last = v.tensor_scalar(hn[s][:, t, :], src[:, t, :], mean_var[s][:, t, 0:1],
                                           rstd[s][:, t:t + 1], ALU.subtract, ALU.mult)
                last.then_inc(hn_made[s], 1)

            def scores(s, it, unit):
                call, first, heads = UNITS[unit]
                mask = mask_n[s] if call == 3 else mask_t[s]
                if call == 0:
                    held_until(dve, dve_passed, turned_taken[s], value(TURNED, it, "mask_t"))
                if call == 1:
                    held_until(dve, dve_passed, masks[s], value(MASKS, it, "mask_t diagonal"))
                if call == 3:
                    held_until(dve, dve_passed, masks[s], value(MASKS, it, "mask_n diagonal"))
                held_until(dve, dve_passed, bcast[s], 5 * it + unit + 1)
                terms = val[s][:, :, D + 1:D + 2] if call in (0, 2) else cols[s][:, :, first:first + heads, 1]
                these = slice(first, first + heads)
                for h in range(first, first + heads):
                    row = halves(s, 0 if h < 2 else 1)[:, h % 2, :]
                    for t in range(T):
                        last = v.tensor_tensor_reduce(out=z[s][:, h, t, :], in0=row, in1=mask[:, t, :], scale=1.0,
                                                      scalar=LOWEST, op0=ALU.add, op1=ALU.max,
                                                      accum_out=row_max[s][:, t, h:h + 1])
                last.then_inc(max_steps[s], 1)
                dve.wait_ge(max_steps[s], 4 * (5 * it + unit) + 1)
                v.tensor_tensor(row_top[s][:, :, these], row_max[s][:, :, these], terms,
                                ALU.add).then_inc(max_steps[s], 1)
                dve.wait_ge(max_steps[s], 4 * (5 * it + unit) + 2)
                v.tensor_scalar(row_low[s][:, :, these], row_top[s][:, :, these], -SLOPE, None,
                                ALU.mult).then_inc(max_steps[s], 1)
                dve.wait_ge(max_steps[s], 4 * (5 * it + unit) + 3)
                v.scalar_tensor_tensor(neg_max[s][:, :, these], row_top[s][:, :, these], -1.0,
                                       row_low[s][:, :, these], ALU.mult, ALU.min).then_inc(max_steps[s], 1)

            def leaky(s, it, unit):
                call, first, heads = UNITS[unit]
                for h in range(first, first + heads):
                    dve.wait_ge(scaled[s], 7 * it + CALLS[call][0] + h + 1)
                    for t in range(T):
                        last = v.scalar_tensor_tensor(z[s][:, h, t, :], z[s][:, h, t, :], col(s, call, t, h, 1),
                                                      pT[s][:, h, t, :], ALU.add, ALU.max)
                    last.then_inc(leaky_done[s], 1)

            def inverse_sums(s, it, call):
                before, heads = CALLS[call]
                dve.wait_ge(exp_done[s], 7 * it + before + heads)
                v.reciprocal(rec[s][:, :, 0:heads], row_sum[s][:, :, 0:heads]).then_inc(rec_made[s], 1)
                dve.wait_ge(rec_made[s], 5 * it + REC_OF[call])

            def take_pT(s, it, n, b, to):
                if n not in BY_ACT:
                    dve.wait_ge(pT_psum[s], 14 * it + n + 1)
                    v.tensor_copy(pT[s][:, to, :, :], halves(s, b)).then_inc(pT_by_dve[s], 1)

            def max1(s, it, h):
                dve.wait_ge(s_psum[s], 8 * it + h + 1)
                v.tensor_reduce(neg_max1[s][:, h, :], halves(s, h % 2), AX.X, ALU.max,
                                negate=True).then_inc(neg1_made[s], 1)

            def add_weighted(s, it, call):
                dve.wait_ge(summed[s], value(SUMMED, it, (None, None, "layer 2b", "layer 3")[call]))
                for t in range(T):
                    last = v.scalar_tensor_tensor(x_run[s][:, t, :], halves(s, 0)[:, t, :], rec[s][:, t, 0:1],
                                                  x_run[s][:, t, :], ALU.mult, ALU.add)
                return last

            def stage(s, it, name, n):
                if name == "stats":
                    statistics(s, it, n)
                elif name == "norm" and n < 3:
                    normalise(s, it, n)
                elif name == "row":
                    scores(s, it, n)
                elif name == "leaky":
                    leaky(s, it, n)
                elif name == "sum0":
                    inverse_sums(s, it, 0)
                    for t in range(T):
                        last = v.tensor_scalar(val[s][:, t, 0:D], val[s][:, t, 0:D], rec[s][:, t, 0:1], None,
                                               ALU.mult)
                    last.then_inc(dve_steps[s], 1)
                elif name == "add0":
                    dve.wait_ge(outputs_taken[s], value(OUTPUTS, it, "slope * layer 0"))
                    v.scalar_tensor_tensor(u[s][:, :, 0:D], halves(s, 0), 1.0, u[s][:, :, 0:D], ALU.mult,
                                           ALU.max).then_inc(dve_steps[s], 1)
                    dve.wait_ge(dve_steps[s], value(DVE_STEPS, it, "leaky 0"))
                    dve.wait_ge(stored[s], 16 * it + 16)
                    v.tensor_tensor(x_run[s][:], x_in[s][:], u[s][:, :, 0:D], ALU.add).then_inc(x_made[s], 1)
                elif name == "qkv":
                    dve.wait_ge(projected[s], value(PROJECTED, it, "k"))
                    dve.wait_ge(prepared[s], value(PREPARED, it, "keys cleared"))
                    for j in range(PER):
                        at = slice(DK * j, DK * (j + 1))
                        last = v.tensor_copy(kT[s][at].rearrange("p (c j) n -> p c j n", j=PER)[:, :, j, :],
                                             halves(s, 0)[at])
                    last.then_inc(dve_steps[s], 1)
                elif name == "scores1":
                    max1(s, it, n)
                elif name == "turn1":
                    take_pT(s, it, n, n % 2, n % 4)
                elif name == "rec1":
                    dve.wait_ge(exp1_done[s], 8 * it + HEADS1)
                    v.reciprocal(inv1[s][:], row_sum1[s][:]).then_inc(dve_steps[s], 1)
                    dve.wait_ge(dve_steps[s], value(DVE_STEPS, it, "1 / sums"))
                    v.tensor_copy(rec1[s][:].rearrange("p t h d -> p (t h) d"),
                                  inv1[s][:].rearrange("p t h -> p (t h)").unsqueeze(2).to_broadcast(
                                      [P, T * HEADS1, DK])).then_inc(rec_made[s], 1)
                elif name == "oT":
                    dve.wait_ge(projected[s], value(PROJECTED, it, "1 / sums"))
                    dve.wait_ge(outputs_taken[s], value(OUTPUTS, it, "layer 1 heads 1"))
                    v.tensor_tensor(oT[s][:], oT[s][:], halves(s, 0), ALU.mult).then_inc(dve_steps[s], 1)
                elif name == "wo":
                    dve.wait_ge(projected[s], value(PROJECTED, it, "wo"))
                    v.tensor_tensor(x_run[s][:], x_run[s][:], halves(s, 1), ALU.add).then_inc(x_made[s], 1)
                elif name == "proj2":
                    dve.wait_ge(projected[s], value(PROJECTED, it, "terms 2"))
                    v.tensor_copy(cols[s][:], bank(s, 1)[:, 0:T * HEADS2 * 2].rearrange(
                        "p (t h v) -> p t h v", t=T, v=2)).then_inc(cols_made[s], 1)
                elif name == "turn2":
                    take_pT(s, it, HEADS1 + n, n % 2, n)
                elif name == "rec2":
                    inverse_sums(s, it, 1)
                elif name == "u":
                    for t in range(T):
                        dve.wait_ge(summed[s], value(SUMMED, it, f"layer 2a tile {t}"))
                        v.tensor_tensor(u[s][:, t, :].rearrange("p (h f) -> p h f", h=HEADS2),
                                        bank(s, t).rearrange("p (h f) -> p h f", h=HEADS2),
                                        rec[s][:, t, :].unsqueeze(2).to_broadcast([P, HEADS2, F2]),
                                        ALU.mult).then_inc(h1_steps[s], 1)
                elif name == "elu":
                    for t in range(T):
                        dve.wait_ge(e_made[s], 2 * it + t + 1)
                        v.scalar_tensor_tensor(u[s][:, t, :], e[s][:, t, :], 1.0, u[s][:, t, :], ALU.min,
                                               ALU.max).then_inc(h1_steps[s], 1)
                elif name in ("turn3", "turn4"):
                    take_pT(s, it, PT_OF[int(name[-1]) - 1], 1, 0)
                    inverse_sums(s, it, int(name[-1]) - 1)
                elif name == "add3":
                    dve.wait_ge(prepared[s], value(PREPARED, it, "x + b2"))
                    add_weighted(s, it, 2).then_inc(x_made[s], 1)
                elif name == "norm":
                    normalise(s, it, 3)
                    dve.wait_ge(hn_made[s], 4 * it + 4)
                    v.tensor_scalar(hn[s][:], hn[s][:], 0.0, None, ALU.max).then_inc(dve_steps[s], 1)
                elif name == "cols4":
                    dve.wait_ge(dve_steps[s], value(DVE_STEPS, it, "relu 3"))
                    for t in range(T):
                        for c in range(2):
                            last = v.tensor_tensor_reduce(out=e[s][:, t, c * D:(c + 1) * D], in0=hn[s][:, t, :],
                                                          in1=w3_bc[:, c, :], scale=1.0, scalar=0.0, op0=ALU.mult,
                                                          op1=ALU.add, accum_out=cols[s][:, t, 0, c:c + 1])
                    last.then_inc(dve_steps[s], 1)
                    dve.wait_ge(dve_steps[s], value(DVE_STEPS, it, "raw terms 3"))
                    v.tensor_scalar(cols[s][:, :, 0, 1], cols[s][:, :, 0, 1], b3_bc[:], None,
                                    ALU.add).then_inc(cols_made[s], 1)
                elif name == "add4":
                    add_weighted(s, it, 3).then_inc(x_made[s], 1)

            walk(dve, "DVE", stage)


_INS = ['x', 'adj', 'L0_gnn_W', 'L0_gnn_a', 'L1_gnn_Wq', 'L1_gnn_Wk', 'L1_gnn_Wv', 'L1_gnn_Wo', 'L2_gnn_W1',
        'L2_gnn_att_src1', 'L2_gnn_att_dst1', 'L2_gnn_b1', 'L2_gnn_W2', 'L2_gnn_att_src2', 'L2_gnn_att_dst2',
        'L2_gnn_b2', 'L3_gnn_attn_w_src', 'L3_gnn_attn_w_dst', 'L3_gnn_attn_b']


def kernel(**inputs):
    import numpy as _np
    import concourse.bacc as _bacc
    from concourse import mybir as _mybir
    from concourse.bass_utils import run_bass_kernel_spmd as _run

    nc = _bacc.Bacc("TRN2", target_bir_lowering=False, num_devices=1)
    arrays, args = {}, []
    for name in _INS:
        a = _np.ascontiguousarray(inputs[name])
        arrays[f"in_{name}"] = a
        args.append(nc.dram_tensor(f"in_{name}", a.shape, _mybir.dt.from_np(a.dtype), kind="ExternalInput").ap())
    shape = arrays["in_x"].shape
    args.append(nc.dram_tensor("out_0", shape, _mybir.dt.float32, kind="ExternalOutput").ap())
    four_graph_layers(nc, *args)
    r = _run(nc, [arrays], core_ids=[0])
    return r.results[0]["out_0"]
```

```python
import concourse.bass as bass
from concourse import mybir
from contextlib import ExitStack


def four_graph_layers(nc, x, adj, w0, a0, wq, wk, wv, wo, w1, att_src1, att_dst1, b1, w2, att_src2,
                      att_dst2, b2, w_src3, w_dst3, b3, out):
    fp32, bf16, i32 = mybir.dt.float32, mybir.dt.bfloat16, mybir.dt.int32
    ALU, ACT = mybir.AluOpType, mybir.ActivationFunctionType

    P = 128
    G, N, D = x.shape
    T = N // P
    C = D // P
    SLOTS = range(4)
    ROUNDS = G // len(SLOTS)
    HEADS1 = 8
    DK = D // HEADS1
    PER = P // DK
    HEADS2 = att_src1.shape[0]
    F2 = att_src1.shape[1]
    FH = HEADS2 * F2
    CH = FH // P
    SLOPE = 0.2
    EPS = 1e-5
    MASKED = -float(2 ** 53)
    LOWEST = -3.0e38
    ONE = D + 2

    with ExitStack() as ctx:
        def sb(name, shape, dt=fp32):
            return ctx.enter_context(nc.sbuf_tensor(name, shape, dt))

        def per_slot(name, shape, dt=fp32):
            return [sb(f"{name}_{s}", shape, dt) for s in SLOTS]

        def sem(name):
            return ctx.enter_context(nc.semaphore(name))

        def sems(name):
            return [sem(f"{name}_{s}") for s in SLOTS]

        ident = sb("ident", [P, P])
        ident16 = sb("ident16", [P, P], bf16)
        w0_sb = sb("w0_sb", [P, C, ONE])
        wq_sb, wk_sb, wv_sb, wo_sb = (sb(n, [P, C, D]) for n in ("wq_sb", "wk_sb", "wv_sb", "wo_sb"))
        w1_sb = sb("w1_sb", [P, C, FH])
        w1_cols = sb("w1_cols", [P, C, HEADS2, 2])
        w2_sb = sb("w2_sb", [P, CH, ONE])
        a0_sb = sb("a0_sb", [P, C, 2])
        att1_sb = sb("att1_sb", [P, HEADS2, 2])
        att2_sb = sb("att2_sb", [P, C, 2])
        b1_bc = sb("b1_bc", [P, FH])
        b2_bc = sb("b2_bc", [P, D])
        w3_bc = sb("w3_bc", [P, 2, D])
        b3_bc = sb("b3_bc", [P, 1])
        minus_one = sb("minus_one", [P, 1])
        minus_half = sb("minus_half", [P, T])

        adj_in = per_slot("adj_in", [P, T, N], i32)
        x_in = per_slot("x_in", [P, T, D])
        x_run = per_slot("x_run", [P, T, D])
        bn = per_slot("bn", [P, T, 6])
        mean_var = per_slot("mean_var", [P, T, 2])
        var_eps = per_slot("var_eps", [P, T])
        rstd = per_slot("rstd", [P, T])
        neg_mean = per_slot("neg_mean", [P, T])
        shift = per_slot("shift", [P, T])
        hn = per_slot("hn", [P, T, D])
        hT = per_slot("hT", [P, C, N])
        mask_n = per_slot("mask_n", [P, T, N], bf16)
        mask_t = per_slot("mask_t", [P, T, N], bf16)
        val = per_slot("val", [P, T, FH])
        cols = per_slot("cols", [P, T, HEADS2, 2])
        z = per_slot("z", [P, 4, T, N])
        row_max = per_slot("row_max", [P, T, HEADS2])
        row_top = per_slot("row_top", [P, T, HEADS2])
        row_low = per_slot("row_low", [P, T, HEADS2])
        neg_max = per_slot("neg_max", [P, T, HEADS2])
        max1 = per_slot("max1", [P, HEADS1, T])
        neg_max1 = per_slot("neg_max1", [P, HEADS1, T])
        row_sum = per_slot("row_sum", [P, T, HEADS2])
        rec = per_slot("rec", [P, T, HEADS2])
        row_sum1 = per_slot("row_sum1", [P, T, HEADS1])
        inv1 = per_slot("inv1", [P, T, HEADS1])
        pT = per_slot("pT", [P, 4, T, N])
        wide = per_slot("wide", [P, 2, T, FH])

        u = [w[:, 0] for w in wide]
        e = [w[:, 1] for w in wide]
        kT = [w[:].rearrange("p a t (b n) -> p (a t b) n", n=N) for w in wide]
        rec1 = [w[:, 0].rearrange("p t f -> p (t f)")[:, 0:T * D].rearrange("p (t h d) -> p t h d", t=T, h=HEADS1)
                for w in wide]
        qT = hn
        oT = hT
        h1T = [m[:, 2:4].rearrange("p h t n -> p (h t) n") for m in z]
        wT_sb = z[0][:, 0:2].rearrange("p h t n -> p h (t n)")

        ps = [ctx.enter_context(nc.psum_tensor(f"ps_{s}", [P, 2, 512], fp32)) for s in SLOTS]

        def bank(s, b):
            return ps[s][:, b, :]

        def col(s, call, t, h, v):
            return val[s][:, t, D + v:D + v + 1] if call in (0, 2) else cols[s][:, t, h, v:v + 1]

        def halves(s, b):
            return ps[s][:, b, :].rearrange("p (t n) -> p t n", t=2)

        consts_in = sem("consts_in")
        ident_made = sem("ident_made")
        setup_psum, setup_sb = sem("setup_psum"), sem("setup_sb")
        setup_done = sem("setup_done")
        loaded, stored = sems("loaded"), sems("stored")
        MASKS = ("mask_n", "mask_t diagonal", "mask_n diagonal")
        masks = sems("masks")
        PREPARED = ("keys cleared", "val + b1", "x + b2")
        prepared = sems("prepared")
        TURNED = ("mask_t", "hT 0", "hT 1", "hT 2", "h1T 0", "h1T 1")
        turned, turned_taken = sems("turned"), sems("turned_taken")
        PROJECTED = ("layer 0", "q", "k", "v", "1 / sums", "wo", "terms 2", "xl 0", "xl 1", "layer 2b")
        projected = sems("projected")
        SUMMED = ("layer 0", "layer 1 heads 0", "layer 1 heads 1", "layer 2a tile 0", "layer 2a tile 1",
                  "layer 2b", "layer 3")
        summed = sems("summed")
        OUTPUTS = ("slope * layer 0", "layer 1 heads 0", "layer 1 heads 1")
        outputs_taken = sems("outputs_taken")
        DVE_STEPS = ("scaled val", "leaky 0", "1 / sums", "oT", "raw terms 3")
        dve_steps = sems("dve_steps")
        X_MADE = ("free", "layer 0", "layer 1", "layer 2")
        x_made = sems("x_made")
        stat_steps = sems("stat_steps")
        rstd_steps, hn_made = sems("rstd_steps"), sems("hn_made")
        cols_made, val_made = sems("cols_made"), sems("val_made")
        bcast = sems("bcast")
        max_steps = sems("max_steps")
        scaled, leaky_done, exp_done = sems("scaled"), sems("leaky_done"), sems("exp_done")
        rec_made = sems("rec_made")
        pT_psum = sems("pT_psum")
        pT_by_act, pT_by_dve = sems("pT_by_act"), sems("pT_by_dve")
        qkv_made = sems("qkv_made")
        s_psum, max1_made = sems("s_psum"), sems("max1_made")
        neg1_made, exp1_done = sems("neg1_made"), sems("exp1_done")
        e_made, h1_steps = sems("e_made"), sems("h1_steps")
        dve_passed, pool_passed = sem("dve_passed"), sem("pool_passed")

        def value(steps, it, step):
            return len(steps) * it + steps.index(step) + 1

        BY_ACT = {1, 3, 5, 7, 9, 11}
        CALLS = ((0, 1), (1, HEADS2), (1 + HEADS2, 1), (2 + HEADS2, 1))
        UNITS = ((0, 0, 1), (1, 0, 2), (1, 2, 2), (2, 0, 1), (3, 0, 1))
        PT_OF = (None, HEADS1, HEADS1 + HEADS2, HEADS1 + HEADS2 + 1)
        REC_OF = (1, 3, 4, 5)

        ALL_PT = HEADS1 + HEADS2 + 2

        def wait_pT(eng, s, it, n):
            by_act = len([m for m in BY_ACT if m <= n])
            if by_act:
                eng.wait_ge(pT_by_act[s], len(BY_ACT) * it + by_act)
            if n + 1 - by_act:
                eng.wait_ge(pT_by_dve[s], (ALL_PT - len(BY_ACT)) * it + n + 1 - by_act)

        def held_until(eng, passed, semaphore, value):
            eng.wait_ge(semaphore, value)
            eng.sem_inc(passed, 1)

        x_v = x.rearrange("g (t p) d -> g p t d", p=P)
        adj_v = adj.rearrange("g (t p) n -> g p t n", p=P)
        out_v = out.rearrange("g (t p) d -> g p t d", p=P)

        LENGTH, BEHIND = 237.57, (0, 59.47, 118.94, 178.41)
        TIMES = {
            "PE": [(4.18, "mask_t", 0), (15.98, "hT", 0), (38.35, "proj0", 0), (41.99, "row", 0), (58.45, "out0", 0),
                    (74.92, "hT", 1), (76.31, "q", 0), (80.26, "k", 0), (88.35, "v", 0), (90.03, "scores1", 0),
                    (93.76, "scores1", 1), (97.24, "turn1", 0), (99.43, "scores1", 2), (101.02, "turn1", 1),
                    (104.63, "scores1", 3), (105.93, "turn1", 2), (113.9, "scores1", 4), (115.03, "turn1", 3),
                    (119.69, "sum1", 0), (121.32, "scores1", 5), (122.44, "turn1", 4), (125.45, "scores1", 6),
                    (127.71, "turn1", 5), (133.07, "scores1", 7), (133.87, "turn1", 6), (139.09, "turn1", 7),
                    (145.99, "sum1", 1), (147.37, "rows1", 0), (150.64, "wo", 0), (159.93, "hT", 2),
                    (161.34, "proj2", 0), (162.86, "row", 1), (163.41, "row", 2), (166.94, "xl", 0),
                    (170.49, "xl", 1), (183.98, "turn2", 0), (184.43, "turn2", 1), (185.83, "turn2", 2),
                    (186.47, "turn2", 3), (188.33, "sum2", 0), (190.1, "sum2", 1), (197.48, "h1T", 0),
                    (198.12, "h1T", 1), (201.44, "proj3", 0), (206.56, "row", 3), (212.1, "turn3", 0),
                    (213.89, "out3", 0), (224.61, "row", 4), (232.25, "turn4", 0), (234.49, "out4", 0)],
            "DVE": [(0, "stats", 0), (42.48, "row", 0), (54.23, "leaky", 0), (56.65, "sum0", 0), (66.44, "add0", 0),
                    (69.62, "stats", 1), (91.57, "scores1", 0), (95.97, "scores1", 1), (98.25, "turn1", 0),
                    (100.64, "scores1", 2), (111.86, "scores1", 3), (112.85, "turn1", 2), (115.21, "scores1", 4),
                    (123.47, "scores1", 5), (124.45, "turn1", 4), (128.09, "scores1", 6), (134.47, "scores1", 7),
                    (136.17, "turn1", 6), (137.7, "rec1", 0), (149.16, "oT", 0), (152.81, "wo", 0),
                    (154.16, "stats", 2), (162.56, "proj2", 0), (164.64, "row", 1), (167.9, "row", 2),
                    (179.48, "leaky", 1), (181.45, "leaky", 2), (184.65, "turn2", 0), (186.79, "turn2", 2),
                    (187.34, "rec2", 0), (190.28, "u", 0), (192.72, "u", 1), (193.32, "elu", 0), (195.07, "elu", 1),
                    (207.02, "row", 3), (209.74, "leaky", 3), (212.88, "turn3", 0), (216.36, "add3", 0),
                    (217.78, "stats", 3), (222.15, "cols4", 0), (226.24, "row", 4), (229.78, "leaky", 4),
                    (233.34, "turn4", 0), (237.04, "add4", 0)],
            "ACT": [(10.26, "mask_t", 0), (10.27, "norm", 0), (16.77, "hT", 0), (40.13, "proj0", 0),
                    (55.15, "exp", 0), (60.4, "out0", 0), (73.05, "norm", 1), (75.63, "hT", 1), (78.72, "q", 0),
                    (82.67, "k", 0), (90.2, "v", 0), (92.9, "scores1", 0), (97.01, "scores1", 1),
                    (102.98, "scores1", 2), (103.9, "turn1", 1), (113.72, "scores1", 3), (116.3, "scores1", 4),
                    (117.51, "turn1", 3), (120.87, "sum1", 0), (126.64, "scores1", 5), (129.99, "scores1", 6),
                    (131.25, "turn1", 5), (136.38, "scores1", 7), (140.37, "turn1", 7), (147.27, "sum1", 1),
                    (157.52, "norm", 2), (160.67, "hT", 2), (169.27, "xl", 0), (172.6, "xl", 1), (181.62, "exp", 1),
                    (183.8, "exp", 2), (185.59, "turn2", 1), (187.54, "turn2", 3), (191.34, "exp_u", 0),
                    (193.5, "exp_u", 1), (199.26, "h1T", 0), (200, "h1T", 1), (205.64, "proj3", 0),
                    (210.69, "exp", 3), (220.65, "norm", 3), (230.98, "exp", 4)],
            "Pool": [(1.43, "masks", 0), (3.6, "stats", 0), (43.8, "scale", 0), (44.59, "diag_t", 0),
                    (68.03, "clear", 0), (71.08, "stats", 1), (135.77, "diag_n", 0), (155.62, "stats", 2),
                    (173.37, "xl", 1), (175.22, "bias2", 0), (176.34, "scale", 1), (178.25, "scale", 2),
                    (208.81, "scale", 3), (219.26, "stats", 3), (227.55, "scale", 4)],
        }

        def fresh(eng, it):
            own = eng.alloc_register()
            eng.reg_add(own, it, 0)
            return eng.snap(own, min_val=0, max_val=ROUNDS)

        def walk(eng, who, stage):
            def turn(it, rounds):
                order = []
                for s in SLOTS:
                    for tau, name, n in TIMES[who]:
                        back = 1 if tau + BEHIND[s] >= LENGTH else 0
                        if back in rounds:
                            order.append((tau + BEHIND[s] - back * LENGTH, s, back, name, n))
                order.sort()
                here = it
                for i, (_, s, back, name, n) in enumerate(order):
                    if i % 24 == 0 and not isinstance(it, int):
                        here = fresh(eng, it)
                    stage(s, here - back if back else here, name, n)

            turn(0, (0,))
            with eng.Fori(1, ROUNDS) as it:
                turn(it, (0, 1))
            turn(ROUNDS, (1,))

        block = ctx.enter_context(nc.Block())

        @block.sync
        def _(sp):
            for dst, src in ((w0_sb[:, :, 0:D], w0), (wq_sb[:], wq), (wk_sb[:], wk), (wv_sb[:], wv),
                             (wo_sb[:], wo), (w1_sb[:], w1), (w2_sb[:, :, 0:D], w2)):
                sp.dma_start(dst, src.rearrange("(c p) n -> p c n", p=P)).then_inc(consts_in, 16)
            with nc.allow_non_contiguous_dma(reason="vectors laid along the partitions, once"):
                for half in range(2):
                    sp.dma_start(a0_sb[:, :, half],
                                 a0[half * D:(half + 1) * D, 0].rearrange("(c p) -> p c", p=P)).then_inc(consts_in, 16)
                sp.dma_start(att1_sb[:, :, 0], att_src1.rearrange("h f -> f h")).then_inc(consts_in, 16)
                sp.dma_start(att1_sb[:, :, 1], att_dst1.rearrange("h f -> f h")).then_inc(consts_in, 16)
                sp.dma_start(att2_sb[:, :, 0], att_src2.rearrange("o (c p) -> p (o c)", p=P)).then_inc(consts_in, 16)
                sp.dma_start(att2_sb[:, :, 1], att_dst2.rearrange("o (c p) -> p (o c)", p=P)).then_inc(consts_in, 16)
            for dst, src in ((b1_bc[:], b1), (b2_bc[:], b2), (w3_bc[:, 0, :], w_dst3), (w3_bc[:, 1, :], w_src3),
                             (b3_bc[:], b3)):
                sp.dma_start(dst, src.partition_broadcast(P)).then_inc(consts_in, 16)

            def graph(view, g):
                return view[g] if isinstance(g, int) else view[bass.ds(g, 1)].squeeze(0)

            def load(g, s):
                sp.dma_start(adj_in[s][:], graph(adj_v, g)).then_inc(loaded[s], 16)
                sp.dma_start(x_in[s][:], graph(x_v, g)).then_inc(loaded[s], 16)

            def store(g, s):
                sp.dma_start(graph(out_v, g), x_run[s][:]).then_inc(stored[s], 16)

            for s in SLOTS:
                sp.sem_inc(stored[s], 16)
                sp.sem_inc(x_made[s], 1)
                load(s, s)
            with sp.Fori(0, ROUNDS - 1) as it:
                for s in SLOTS:
                    sp.wait_ge(masks[s], value(MASKS, it, "mask_n"))
                    sp.wait_ge(x_made[s], value(X_MADE, it, "layer 0"))
                    load(len(SLOTS) * it + (len(SLOTS) + s), s)
                for s in SLOTS:
                    sp.wait_ge(x_made[s], value(X_MADE, it, "free") + len(X_MADE))
                    store(len(SLOTS) * it + s, s)
            for s in SLOTS:
                sp.wait_ge(x_made[s], value(X_MADE, ROUNDS, "free"))
                store(G - len(SLOTS) + s, s)
            for s in SLOTS:
                sp.wait_ge(stored[s], 16 * (ROUNDS + 1))

        @block.gpsimd
        def _(pool):
            nc.gpsimd.memset(ident[:], 0.0).then_inc(ident_made, 1)
            nc.gpsimd.memset(minus_one[:], -1.0)
            nc.gpsimd.memset(minus_half[:], -0.5)
            pool.wait_ge(ident_made, 1)
            nc.gpsimd.affine_select(out=ident[:], in_=ident[:], compare_op=ALU.not_equal, fill=1.0, base=0,
                                    pattern=[[-1, P]], channel_multiplier=1).then_inc(ident_made, 1)
            pool.wait_ge(ident_made, 2)
            nc.gpsimd.tensor_copy(ident16[:], ident[:]).then_inc(ident_made, 1)

            def inverse_std(s, it, layer):
                held_until(pool, pool_passed, stat_steps[s], 16 * it + 4 * layer + 4)
                nc.gpsimd.tensor_scalar(var_eps[s][:], mean_var[s][:, :, 1], EPS, 1.0, ALU.add,
                                        ALU.mult)
                nc.gpsimd.tensor_scalar(neg_mean[s][:], mean_var[s][:, :, 0], -1.0, 0.0, ALU.mult,
                                        ALU.add).then_inc(rstd_steps[s], 1)
                pool.wait_ge(rstd_steps[s], 12 * it + 3 * layer + 1)
                nc.gpsimd.tensor_tensor(rstd[s][:], var_eps[s][:], minus_half[:], ALU.pow).then_inc(rstd_steps[s], 1)
                pool.wait_ge(rstd_steps[s], 12 * it + 3 * layer + 2)
                nc.gpsimd.tensor_tensor(shift[s][:], neg_mean[s][:], rstd[s][:], ALU.mult).then_inc(rstd_steps[s], 1)

            def open_diagonal(s, mask):
                for t in range(T):
                    v = mask[:, t, t * P:(t + 1) * P]
                    last = nc.gpsimd.affine_select(out=v, in_=v, compare_op=ALU.not_equal, fill=0.0, base=0,
                                                   pattern=[[-1, P]], channel_multiplier=1)
                last.then_inc(masks[s], 1)

            def scale_scores(s, it, unit):
                call, first, heads = UNITS[unit]
                held_until(pool, pool_passed, max_steps[s], 4 * (5 * it + unit) + 1)
                for h in range(first, first + heads):
                    for t in range(T):
                        last = nc.gpsimd.tensor_scalar(pT[s][:, h, t, :], z[s][:, h, t, :],
                                                       col(s, call, t, h, 1), SLOPE, ALU.add, ALU.mult)
                    last.then_inc(scaled[s], 1)

            def stage(s, it, name, n):
                if name == "masks":
                    held_until(pool, pool_passed, x_made[s], value(X_MADE, it, "free"))
                    held_until(pool, pool_passed, loaded[s], 32 * it + 32)
                    nc.gpsimd.tensor_scalar(mask_n[s][:], adj_in[s][:], 0, MASKED, ALU.is_le,
                                            ALU.mult).then_inc(masks[s], 1)
                elif name == "stats":
                    inverse_std(s, it, n)
                elif name == "scale":
                    scale_scores(s, it, n)
                elif name == "clear":
                    held_until(pool, pool_passed, x_made[s], value(X_MADE, it, "layer 0"))
                    nc.gpsimd.memset(wide[s][:], 0.0).then_inc(prepared[s], 1)
                elif name == "xl":
                    pool.wait_ge(val_made[s], 4 * it + 3)
                    nc.gpsimd.tensor_tensor(val[s][:], val[s][:], b1_bc[:].unsqueeze(1).to_broadcast([P, T, FH]),
                                            ALU.add).then_inc(prepared[s], 1)
                elif name == "bias2":
                    pool.wait_ge(hn_made[s], 4 * it + 3)
                    nc.gpsimd.tensor_tensor(x_run[s][:], x_run[s][:], b2_bc[:].unsqueeze(1).to_broadcast([P, T, D]),
                                            ALU.add).then_inc(prepared[s], 1)
                elif name == "diag_t":
                    open_diagonal(s, mask_t[s])
                elif name == "diag_n":
                    held_until(pool, pool_passed, neg1_made[s], 8 * it + HEADS1)
                    open_diagonal(s, mask_n[s])

            walk(pool, "Pool", stage)

        @block.tensor
        def _(pe):
            mm, tr = nc.tensor.matmul, nc.tensor.transpose

            pe.wait_ge(consts_in, 16 * 18)
            pe.wait_ge(ident_made, 3)
            for f in range(C):
                for c in range(C):
                    last = tr(bank(0, f)[:, c * P:(c + 1) * P], w0_sb[:, c, f * P:(f + 1) * P], ident[:])
            last.then_inc(setup_psum, 1)
            pe.wait_ge(setup_sb, 1)
            for c in range(C):
                for f in range(C):
                    last = mm(bank(1, 0)[:, 2 * c:2 * c + 2], wT_sb[:, f, c * P:(c + 1) * P], a0_sb[:, f, :],
                              start=(f == 0), stop=(f == C - 1))
            last.then_inc(setup_psum, 1)
            for h in range(HEADS2):
                pe.wait_ge(setup_sb, 2 + h)
                for c in range(C):
                    last = tr(bank(0, 0)[:, c * P:(c + 1) * P], w1_sb[:, c, h * F2:(h + 1) * F2], ident[:])
                last.then_inc(setup_psum, 1)
                pe.wait_ge(setup_sb, 3 + h)
                for c in range(C):
                    last = mm(bank(1, 1)[:, (c * HEADS2 + h) * 2:(c * HEADS2 + h) * 2 + 2],
                              wT_sb[:, 0, c * P:(c + 1) * P], att1_sb[:, h, :], start=True, stop=True)
            last.then_inc(setup_psum, 1)
            for f in range(C):
                for c in range(CH):
                    last = tr(bank(2, f)[:, c * P:(c + 1) * P], w2_sb[:, c, f * P:(f + 1) * P], ident[:])
            last.then_inc(setup_psum, 1)
            pe.wait_ge(setup_sb, 4 + HEADS2)
            for c in range(CH):
                for f in range(C):
                    last = mm(bank(1, 0)[:, 2 * c:2 * c + 2], wT_sb[:, f, c * P:(c + 1) * P], att2_sb[:, f, :],
                              start=(f == 0), stop=(f == C - 1))
            last.then_inc(setup_psum, 1)
            pe.wait_ge(setup_done, 1)

            def transpose_h(s, it, layer):
                pe.wait_ge(hn_made[s], 4 * it + layer + 1)
                for c in range(C):
                    for t in range(T):
                        last = tr(halves(s, 0)[:, c, t * P:(t + 1) * P], hn[s][:, t, c * P:(c + 1) * P], ident[:])
                last.then_inc(turned[s], 1)

            def project(s, left, n_in, w, width):
                for t in range(T):
                    for c in range(n_in):
                        last = mm(bank(s, t)[:, 0:width], left[:, c, t * P:(t + 1) * P], w[:, c, :],
                                  start=(c == 0), stop=(c == n_in - 1))
                return last

            def broadcast_scores(s, it, unit):
                call, first, heads = UNITS[unit]
                if call in (0, 2):
                    pe.wait_ge(val_made[s], 4 * it + (1, None, 4)[call])
                else:
                    pe.wait_ge(cols_made[s], 2 * it + (1 if call == 1 else 2))
                for h in range(first, first + heads):
                    to = halves(s, 0 if h < 2 else 1)[:, h % 2, :]
                    for t in range(T):
                        last = tr(to[:, t * P:(t + 1) * P], col(s, call, t, h, 0).to_broadcast([P, P]), ident[:])
                last.then_inc(bcast[s], 1)

            def transpose_p(s, b, h):
                for m in range(T):
                    for t in range(T):
                        last = tr(halves(s, b)[:, m, t * P:(t + 1) * P], z[s][:, h, t, m * P:(m + 1) * P], ident[:])
                last.then_inc(pT_psum[s], 1)

            def scores1(s, it, h):
                f = h // PER
                if h >= 2:
                    wait_pT(pe, s, it, h - 2)
                if h == PER + 1:
                    pe.wait_ge(outputs_taken[s], value(OUTPUTS, it, "layer 1 heads 0"))
                for t in range(T):
                    last = mm(halves(s, h % 2)[:, t, :], qT[s][:, f, t * P:(t + 1) * P], kT[s][:, h, :],
                              start=True, stop=True)
                last.then_inc(s_psum[s], 1)

            def weighted(s, it, call, rows):
                wait_pT(pe, s, it, PT_OF[call])
                for d in range(T):
                    for m in range(T):
                        last = mm(halves(s, 0)[:, d, :], pT[s][:, 0, m, d * P:(d + 1) * P], rows[:, m, 0:D],
                                  start=(m == 0), stop=(m == T - 1))
                last.then_inc(summed[s], 1)

            def stage(s, it, name, n):
                if name == "mask_t":
                    pe.wait_ge(masks[s], value(MASKS, it, "mask_n"))
                    to = bank(s, 1).bitcast(bf16)
                    for t in range(T):
                        for r in range(T):
                            last = tr(to[:, t * N + r * P:t * N + (r + 1) * P], mask_n[s][:, r, t * P:(t + 1) * P],
                                      ident16[:])
                    last.then_inc(turned[s], 1)
                elif name == "hT":
                    transpose_h(s, it, n)
                elif name == "proj0":
                    pe.wait_ge(turned_taken[s], value(TURNED, it, "hT 0"))
                    pe.wait_ge(turned_taken[s], value(TURNED, it, "mask_t"))
                    project(s, hT[s], C, w0_sb, ONE).then_inc(projected[s], 1)
                elif name == "row":
                    broadcast_scores(s, it, n)
                elif name == "out0":
                    pe.wait_ge(exp_done[s], 7 * it + 1)
                    pe.wait_ge(dve_steps[s], value(DVE_STEPS, it, "scaled val"))
                    for i in range(T):
                        for j in range(T):
                            last = mm(halves(s, 0)[:, i, :], z[s][:, 0, j, i * P:(i + 1) * P], val[s][:, j, 0:D],
                                      start=(j == 0), stop=(j == T - 1))
                    last.then_inc(summed[s], 1)
                elif name in ("q", "k"):
                    pe.wait_ge(turned_taken[s], value(TURNED, it, "hT 1"))
                    w, b = (wq_sb, 1) if name == "q" else (wk_sb, 0)
                    for f in range(C):
                        for c in range(C):
                            last = mm(halves(s, b)[:, f, :], w[:, c, f * P:(f + 1) * P], hT[s][:, c, :],
                                      start=(c == 0), stop=(c == C - 1))
                    last.then_inc(projected[s], 1)
                elif name == "v":
                    pe.wait_ge(qkv_made[s], 3 * it + 1)
                    for t in range(T):
                        for c in range(C):
                            last = mm(halves(s, 1)[:, t, :], hT[s][:, c, t * P:(t + 1) * P], wv_sb[:, c, :],
                                      start=(c == 0), stop=(c == C - 1))
                    last.then_inc(projected[s], 1)
                elif name == "scores1":
                    if n == 0:
                        pe.wait_ge(qkv_made[s], 3 * it + 2)
                    if n == 1:
                        pe.wait_ge(qkv_made[s], 3 * it + 3)
                    scores1(s, it, n)
                elif name == "turn1":
                    pe.wait_ge(exp1_done[s], 8 * it + n + 1)
                    transpose_p(s, n % 2, n % 4)
                elif name == "sum1":
                    wait_pT(pe, s, it, PER * (n + 1) - 1)
                    for m in range(T):
                        for j in range(PER):
                            h = PER * n + j
                            last = mm(halves(s, 1)[DK * j:DK * (j + 1), 0, :], val[s][:, m, h * DK:(h + 1) * DK],
                                      pT[s][:, j, m, :], start=(m == 0), stop=(m == T - 1))
                    last.then_inc(summed[s], 1)
                elif name == "rows1":
                    pe.wait_ge(rec_made[s], 5 * it + 2)
                    for f in range(C):
                        for t in range(T):
                            last = tr(halves(s, 0)[:, f, t * P:(t + 1) * P],
                                      rec1[s][:, t, PER * f:PER * (f + 1), :].rearrange("p h d -> p (h d)"), ident[:])
                    last.then_inc(projected[s], 1)
                elif name == "wo":
                    pe.wait_ge(dve_steps[s], value(DVE_STEPS, it, "oT"))
                    for t in range(T):
                        for c in range(C):
                            last = mm(halves(s, 1)[:, t, :], oT[s][:, c, t * P:(t + 1) * P], wo_sb[:, c, :],
                                      start=(c == 0), stop=(c == C - 1))
                    last.then_inc(projected[s], 1)
                elif name == "proj2":
                    pe.wait_ge(turned_taken[s], value(TURNED, it, "hT 2"))
                    for t in range(T):
                        for c in range(C):
                            last = mm(bank(s, 1)[:, t * 2 * HEADS2:(t + 1) * 2 * HEADS2],
                                      hT[s][:, c, t * P:(t + 1) * P], w1_cols[:, c, :, :].rearrange("p h v -> p (h v)"),
                                      start=(c == 0), stop=(c == C - 1))
                    last.then_inc(projected[s], 1)
                elif name == "xl":
                    pe.wait_ge(max_steps[s], 4 * (5 * it + n + 1) + 1)
                    for c in range(C):
                        last = mm(bank(s, n), hT[s][:, c, n * P:(n + 1) * P], w1_sb[:, c, :],
                                  start=(c == 0), stop=(c == C - 1))
                    last.then_inc(projected[s], 1)
                elif name == "turn2":
                    pe.wait_ge(exp_done[s], 7 * it + 2 + n)
                    if n < 2:
                        pe.wait_ge(val_made[s], 4 * it + 2 + n)
                    else:
                        wait_pT(pe, s, it, HEADS1 + n - 2)
                    transpose_p(s, n % 2, n)
                elif name == "sum2":
                    pe.wait_ge(prepared[s], value(PREPARED, it, "val + b1"))
                    wait_pT(pe, s, it, HEADS1 + HEADS2 - 1)
                    for h in range(HEADS2):
                        for m in range(T):
                            last = mm(bank(s, n)[:, h * F2:(h + 1) * F2], pT[s][:, h, m, n * P:(n + 1) * P],
                                      val[s][:, m, h * F2:(h + 1) * F2], start=(m == 0), stop=(m == T - 1))
                    last.then_inc(summed[s], 1)
                elif name == "h1T":
                    pe.wait_ge(h1_steps[s], 4 * it + 2 * T)
                    for c in range(CH // 2):
                        for t in range(T):
                            last = tr(halves(s, n)[:, c, t * P:(t + 1) * P],
                                      u[s][:, t, (CH // 2 * n + c) * P:(CH // 2 * n + c + 1) * P], ident[:])
                    last.then_inc(turned[s], 1)
                elif name == "proj3":
                    pe.wait_ge(turned_taken[s], value(TURNED, it, "h1T 1"))
                    project(s, h1T[s], CH, w2_sb, ONE).then_inc(projected[s], 1)
                elif name in ("turn3", "turn4"):
                    pe.wait_ge(exp_done[s], 7 * it + 3 + int(name[-1]))
                    transpose_p(s, 1, 0)
                elif name == "out3":
                    weighted(s, it, 2, val[s])
                elif name == "out4":
                    weighted(s, it, 3, hn[s])

            walk(pe, "PE", stage)

        @block.scalar
        def _(act):
            fn = nc.scalar.activation

            def softmax(s, it, unit):
                call, first, heads = UNITS[unit]
                act.wait_ge(max_steps[s], 4 * (5 * it + unit) + 4)
                for h in range(first, first + heads):
                    act.wait_ge(leaky_done[s], 7 * it + CALLS[call][0] + h + 1)
                    for t in range(T):
                        last = fn(z[s][:, h, t, :], z[s][:, h, t, :], ACT.Exp, bias=neg_max[s][:, t, h:h + 1],
                                  accum_out=row_sum[s][:, t, h:h + 1])
                    last.then_inc(exp_done[s], 1)

            def take_pT(s, it, n, b, to):
                if n in BY_ACT:
                    act.wait_ge(pT_psum[s], 14 * it + n + 1)
                    fn(pT[s][:, to, :, :], halves(s, b), ACT.Copy).then_inc(pT_by_act[s], 1)

            def exp1(s, it, h):
                act.wait_ge(neg1_made[s], 8 * it + h + 1)
                for t in range(T):
                    last = fn(z[s][:, h % 4, t, :], z[s][:, h % 4, t, :], ACT.Exp,
                              bias=neg_max1[s][:, h, t:t + 1], accum_out=row_sum1[s][:, t, h:h + 1])
                last.then_inc(exp1_done[s], 1)

            def stage(s, it, name, n):
                if name == "mask_t":
                    act.wait_ge(turned[s], value(TURNED, it, "mask_t"))
                    fn(mask_t[s][:].rearrange("p t n -> p (t n)"), bank(s, 1).bitcast(bf16)[:, 0:T * N],
                       ACT.Copy).then_inc(turned_taken[s], 1)
                elif name == "norm":
                    if n == 0:
                        act.wait_ge(x_made[s], value(X_MADE, it, "free"))
                    act.wait_ge(rstd_steps[s], 12 * it + 3 * n + 3)
                    for t in range(T):
                        last = fn(hn[s][:, t, :], (x_run[s] if n else x_in[s])[:, t, :], ACT.Relu,
                                  scale=rstd[s][:, t:t + 1], bias=shift[s][:, t:t + 1])
                    last.then_inc(hn_made[s], 1)
                elif name == "hT":
                    act.wait_ge(turned[s], value(TURNED, it, f"hT {n}"))
                    fn(hT[s][:], halves(s, 0), ACT.Copy).then_inc(turned_taken[s], 1)
                elif name == "exp":
                    softmax(s, it, n)
                elif name in ("proj0", "proj3"):
                    act.wait_ge(projected[s], value(PROJECTED, it, "layer 0" if name == "proj0" else "layer 2b"))
                    fn(val[s][:, :, 0:ONE], ps[s][:, :, 0:ONE], ACT.Copy).then_inc(val_made[s], 1)
                elif name == "xl":
                    act.wait_ge(projected[s], value(PROJECTED, it, f"xl {n}"))
                    fn(val[s][:, n, :], bank(s, n), ACT.Copy).then_inc(val_made[s], 1)
                elif name == "q":
                    act.wait_ge(projected[s], value(PROJECTED, it, "q"))
                    fn(qT[s][:], halves(s, 1), ACT.Copy, scale=float(DK) ** -0.5).then_inc(qkv_made[s], 1)
                elif name == "k":
                    act.wait_ge(projected[s], value(PROJECTED, it, "k"))
                    act.wait_ge(prepared[s], value(PREPARED, it, "keys cleared"))
                    for j in range(PER):
                        at = slice(DK * j, DK * (j + 1))
                        last = fn(kT[s][at].rearrange("p (c j) n -> p c j n", j=PER)[:, :, j, :], halves(s, 0)[at],
                                  ACT.Copy)
                    last.then_inc(qkv_made[s], 1)
                elif name == "v":
                    act.wait_ge(projected[s], value(PROJECTED, it, "v"))
                    fn(val[s][:, :, 0:D], halves(s, 1), ACT.Copy).then_inc(qkv_made[s], 1)
                elif name == "scores1":
                    exp1(s, it, n)
                elif name == "turn1":
                    take_pT(s, it, n, n % 2, n % 4)
                elif name == "out0":
                    act.wait_ge(summed[s], value(SUMMED, it, "layer 0"))
                    fn(u[s][:, :, 0:D], halves(s, 0), ACT.Copy, scale=SLOPE).then_inc(outputs_taken[s], 1)
                elif name == "sum1":
                    act.wait_ge(summed[s], value(SUMMED, it, f"layer 1 heads {n}"))
                    fn(oT[s][:, n, :], halves(s, 1)[:, 0, :], ACT.Relu).then_inc(outputs_taken[s], 1)
                elif name == "turn2":
                    take_pT(s, it, HEADS1 + n, n % 2, n)
                elif name == "exp_u":
                    act.wait_ge(h1_steps[s], 4 * it + n + 1)
                    fn(e[s][:, n, :], u[s][:, n, :], ACT.Exp, bias=minus_one[:]).then_inc(e_made[s], 1)
                elif name == "h1T":
                    act.wait_ge(turned[s], value(TURNED, it, f"h1T {n}"))
                    fn(h1T[s][:, CH // 2 * n:CH // 2 * (n + 1), :], halves(s, n), ACT.Identity,
                       bias=minus_one[:]).then_inc(turned_taken[s], 1)
                elif name in ("turn3", "turn4"):
                    take_pT(s, it, PT_OF[int(name[-1]) - 1], 1, 0)

            walk(act, "ACT", stage)

        @block.vector
        def _(dve):
            v = nc.vector
            dve.wait_ge(setup_psum, 1)
            v.tensor_copy(wT_sb[:, :, 0:D], ps[0][:, 0:2, 0:D]).then_inc(setup_sb, 1)
            dve.wait_ge(setup_psum, 2)
            v.tensor_copy(w0_sb[:, :, D:D + 2],
                          bank(1, 0)[:, 0:2 * C].rearrange("p (c v) -> p c v", v=2)).then_inc(setup_sb, 1)
            for h in range(HEADS2):
                dve.wait_ge(setup_psum, 3 + h)
                v.tensor_copy(wT_sb[:, 0, 0:D], bank(0, 0)[:, 0:D]).then_inc(setup_sb, 1)
            dve.wait_ge(setup_psum, 3 + HEADS2)
            v.tensor_copy(w1_cols[:].rearrange("p c h v -> p (c h v)"),
                          bank(1, 1)[:, 0:C * HEADS2 * 2]).then_inc(setup_sb, 1)
            dve.wait_ge(setup_psum, 4 + HEADS2)
            v.tensor_copy(wT_sb[:, :, 0:FH], ps[2][:, :, 0:FH]).then_inc(setup_sb, 1)
            dve.wait_ge(consts_in, 16 * 18)
            v.tensor_scalar(b1_bc[:], b1_bc[:], 1.0, None, ALU.add)
            dve.wait_ge(setup_psum, 5 + HEADS2)
            v.tensor_copy(w2_sb[:, :, D:D + 2],
                          bank(1, 0)[:, 0:2 * CH].rearrange("p (c v) -> p c v", v=2)).then_inc(setup_done, 1)
            dve.wait_ge(setup_done, 1)

            def statistics(s, it, layer):
                src = x_run[s] if layer else x_in[s]
                if layer:
                    dve.wait_ge(x_made[s], value(X_MADE, it, f"layer {layer - 1}"))
                else:
                    dve.wait_ge(loaded[s], 32 * it + 32)
                for t in range(T):
                    v.bn_stats(bn[s][:, t, :], src[:, t, :]).then_inc(stat_steps[s], 1)
                for t in range(T):
                    held_until(dve, dve_passed, stat_steps[s], 16 * it + 4 * layer + t + 1)
                    v.bn_aggr(mean_var[s][:, t, :], bn[s][:, t, :]).then_inc(stat_steps[s], 1)

            def scores(s, it, unit):
                call, first, heads = UNITS[unit]
                mask = mask_n[s] if call == 3 else mask_t[s]
                if call == 0:
                    held_until(dve, dve_passed, turned_taken[s], value(TURNED, it, "mask_t"))
                if call == 1:
                    held_until(dve, dve_passed, masks[s], value(MASKS, it, "mask_t diagonal"))
                if call == 3:
                    held_until(dve, dve_passed, masks[s], value(MASKS, it, "mask_n diagonal"))
                held_until(dve, dve_passed, bcast[s], 5 * it + unit + 1)
                terms = val[s][:, :, D + 1:D + 2] if call in (0, 2) else cols[s][:, :, first:first + heads, 1]
                these = slice(first, first + heads)
                for h in range(first, first + heads):
                    row = halves(s, 0 if h < 2 else 1)[:, h % 2, :]
                    for t in range(T):
                        last = v.tensor_tensor_reduce(out=z[s][:, h, t, :], in0=row, in1=mask[:, t, :], scale=1.0,
                                                      scalar=LOWEST, op0=ALU.add, op1=ALU.max,
                                                      accum_out=row_max[s][:, t, h:h + 1])
                last.then_inc(max_steps[s], 1)
                dve.wait_ge(max_steps[s], 4 * (5 * it + unit) + 1)
                v.tensor_tensor(row_top[s][:, :, these], row_max[s][:, :, these], terms,
                                ALU.add).then_inc(max_steps[s], 1)
                dve.wait_ge(max_steps[s], 4 * (5 * it + unit) + 2)
                v.tensor_scalar(row_low[s][:, :, these], row_top[s][:, :, these], -SLOPE, None,
                                ALU.mult).then_inc(max_steps[s], 1)
                dve.wait_ge(max_steps[s], 4 * (5 * it + unit) + 3)
                v.scalar_tensor_tensor(neg_max[s][:, :, these], row_top[s][:, :, these], -1.0,
                                       row_low[s][:, :, these], ALU.mult, ALU.min).then_inc(max_steps[s], 1)

            def leaky(s, it, unit):
                call, first, heads = UNITS[unit]
                for h in range(first, first + heads):
                    dve.wait_ge(scaled[s], 7 * it + CALLS[call][0] + h + 1)
                    for t in range(T):
                        last = v.scalar_tensor_tensor(z[s][:, h, t, :], z[s][:, h, t, :], col(s, call, t, h, 1),
                                                      pT[s][:, h, t, :], ALU.add, ALU.max)
                    last.then_inc(leaky_done[s], 1)

            def inverse_sums(s, it, call):
                before, heads = CALLS[call]
                dve.wait_ge(exp_done[s], 7 * it + before + heads)
                v.reciprocal(rec[s][:, :, 0:heads], row_sum[s][:, :, 0:heads]).then_inc(rec_made[s], 1)
                dve.wait_ge(rec_made[s], 5 * it + REC_OF[call])

            def take_pT(s, it, n, b, to):
                if n not in BY_ACT:
                    dve.wait_ge(pT_psum[s], 14 * it + n + 1)
                    v.tensor_copy(pT[s][:, to, :, :], halves(s, b)).then_inc(pT_by_dve[s], 1)

            def mask1(s, it, h):
                if h >= 4:
                    held_until(dve, dve_passed, pT_psum[s], 14 * it + h - 3)
                held_until(dve, dve_passed, s_psum[s], 8 * it + h + 1)
                for t in range(T):
                    last = v.tensor_tensor_reduce(out=z[s][:, h % 4, t, :], in0=halves(s, h % 2)[:, t, :],
                                                  in1=mask_n[s][:, t, :], scale=1.0, scalar=LOWEST, op0=ALU.add,
                                                  op1=ALU.max, accum_out=max1[s][:, h, t:t + 1])
                last.then_inc(max1_made[s], 1)
                dve.wait_ge(max1_made[s], 8 * it + h + 1)
                v.tensor_scalar(neg_max1[s][:, h, :], max1[s][:, h, :], -1.0, None, ALU.mult).then_inc(neg1_made[s], 1)

            def add_weighted(s, it, call):
                dve.wait_ge(summed[s], value(SUMMED, it, (None, None, "layer 2b", "layer 3")[call]))
                for t in range(T):
                    last = v.scalar_tensor_tensor(x_run[s][:, t, :], halves(s, 0)[:, t, :], rec[s][:, t, 0:1],
                                                  x_run[s][:, t, :], ALU.mult, ALU.add)
                return last

            def stage(s, it, name, n):
                if name == "stats":
                    statistics(s, it, n)
                elif name == "row":
                    scores(s, it, n)
                elif name == "leaky":
                    leaky(s, it, n)
                elif name == "sum0":
                    inverse_sums(s, it, 0)
                    for t in range(T):
                        last = v.tensor_scalar(val[s][:, t, 0:D], val[s][:, t, 0:D], rec[s][:, t, 0:1], None,
                                               ALU.mult)
                    last.then_inc(dve_steps[s], 1)
                elif name == "add0":
                    dve.wait_ge(outputs_taken[s], value(OUTPUTS, it, "slope * layer 0"))
                    v.scalar_tensor_tensor(u[s][:, :, 0:D], halves(s, 0), 1.0, u[s][:, :, 0:D], ALU.mult,
                                           ALU.max).then_inc(dve_steps[s], 1)
                    dve.wait_ge(dve_steps[s], value(DVE_STEPS, it, "leaky 0"))
                    dve.wait_ge(stored[s], 16 * it + 16)
                    v.tensor_tensor(x_run[s][:], x_in[s][:], u[s][:, :, 0:D], ALU.add).then_inc(x_made[s], 1)
                elif name == "scores1":
                    mask1(s, it, n)
                elif name == "turn1":
                    take_pT(s, it, n, n % 2, n % 4)
                elif name == "rec1":
                    dve.wait_ge(exp1_done[s], 8 * it + HEADS1)
                    v.reciprocal(inv1[s][:], row_sum1[s][:]).then_inc(dve_steps[s], 1)
                    dve.wait_ge(dve_steps[s], value(DVE_STEPS, it, "1 / sums"))
                    v.tensor_copy(rec1[s][:].rearrange("p t h d -> p (t h) d"),
                                  inv1[s][:].rearrange("p t h -> p (t h)").unsqueeze(2).to_broadcast(
                                      [P, T * HEADS1, DK])).then_inc(rec_made[s], 1)
                elif name == "oT":
                    dve.wait_ge(projected[s], value(PROJECTED, it, "1 / sums"))
                    dve.wait_ge(outputs_taken[s], value(OUTPUTS, it, "layer 1 heads 1"))
                    v.tensor_tensor(oT[s][:], oT[s][:], halves(s, 0), ALU.mult).then_inc(dve_steps[s], 1)
                elif name == "wo":
                    dve.wait_ge(projected[s], value(PROJECTED, it, "wo"))
                    v.tensor_tensor(x_run[s][:], x_run[s][:], halves(s, 1), ALU.add).then_inc(x_made[s], 1)
                elif name == "proj2":
                    dve.wait_ge(projected[s], value(PROJECTED, it, "terms 2"))
                    v.tensor_copy(cols[s][:], bank(s, 1)[:, 0:T * HEADS2 * 2].rearrange(
                        "p (t h v) -> p t h v", t=T, v=2)).then_inc(cols_made[s], 1)
                elif name == "turn2":
                    take_pT(s, it, HEADS1 + n, n % 2, n)
                elif name == "rec2":
                    inverse_sums(s, it, 1)
                elif name == "u":
                    dve.wait_ge(summed[s], value(SUMMED, it, f"layer 2a tile {n}"))
                    v.tensor_tensor(u[s][:, n, :].rearrange("p (h f) -> p h f", h=HEADS2),
                                    bank(s, n).rearrange("p (h f) -> p h f", h=HEADS2),
                                    rec[s][:, n, :].unsqueeze(2).to_broadcast([P, HEADS2, F2]),
                                    ALU.mult).then_inc(h1_steps[s], 1)
                elif name == "elu":
                    dve.wait_ge(e_made[s], 2 * it + n + 1)
                    v.scalar_tensor_tensor(u[s][:, n, :], e[s][:, n, :], 1.0, u[s][:, n, :], ALU.min,
                                           ALU.max).then_inc(h1_steps[s], 1)
                elif name in ("turn3", "turn4"):
                    take_pT(s, it, PT_OF[int(name[-1]) - 1], 1, 0)
                    inverse_sums(s, it, int(name[-1]) - 1)
                elif name == "add3":
                    dve.wait_ge(prepared[s], value(PREPARED, it, "x + b2"))
                    add_weighted(s, it, 2).then_inc(x_made[s], 1)
                elif name == "cols4":
                    held_until(dve, dve_passed, hn_made[s], 4 * it + 4)
                    for t in range(T):
                        for c in range(2):
                            last = v.tensor_tensor_reduce(out=e[s][:, t, c * D:(c + 1) * D], in0=hn[s][:, t, :],
                                                          in1=w3_bc[:, c, :], scale=1.0, scalar=0.0, op0=ALU.mult,
                                                          op1=ALU.add, accum_out=cols[s][:, t, 0, c:c + 1])
                    last.then_inc(dve_steps[s], 1)
                    dve.wait_ge(dve_steps[s], value(DVE_STEPS, it, "raw terms 3"))
                    v.tensor_scalar(cols[s][:, :, 0, 1], cols[s][:, :, 0, 1], b3_bc[:], None,
                                    ALU.add).then_inc(cols_made[s], 1)
                elif name == "add4":
                    add_weighted(s, it, 3).then_inc(x_made[s], 1)

            walk(dve, "DVE", stage)


_INS = ['x', 'adj', 'L0_gnn_W', 'L0_gnn_a', 'L1_gnn_Wq', 'L1_gnn_Wk', 'L1_gnn_Wv', 'L1_gnn_Wo', 'L2_gnn_W1',
        'L2_gnn_att_src1', 'L2_gnn_att_dst1', 'L2_gnn_b1', 'L2_gnn_W2', 'L2_gnn_att_src2', 'L2_gnn_att_dst2',
        'L2_gnn_b2', 'L3_gnn_attn_w_src', 'L3_gnn_attn_w_dst', 'L3_gnn_attn_b']


def kernel(**inputs):
    import numpy as _np
    import concourse.bacc as _bacc
    from concourse import mybir as _mybir
    from concourse.bass_utils import run_bass_kernel_spmd as _run

    nc = _bacc.Bacc("TRN2", target_bir_lowering=False, num_devices=1)
    arrays, args = {}, []
    for name in _INS:
        a = _np.ascontiguousarray(inputs[name])
        arrays[f"in_{name}"] = a
        args.append(nc.dram_tensor(f"in_{name}", a.shape, _mybir.dt.from_np(a.dtype), kind="ExternalInput").ap())
    shape = arrays["in_x"].shape
    args.append(nc.dram_tensor("out_0", shape, _mybir.dt.float32, kind="ExternalOutput").ap())
    four_graph_layers(nc, *args)
    r = _run(nc, [arrays], core_ids=[0])
    return r.results[0]["out_0"]
```
